# Optimizing a Trainium2 kernel written in Bass

```python
import numpy as np
import jax
import jax.numpy as jnp

def _softmax(x, axis=-1):
    return jax.nn.softmax(x, axis=axis)

def _gelu(x):
    return jax.nn.gelu(x, approximate=True)

def _silu(x):
    return jax.nn.silu(x)

def _sigmoid(x):
    return jax.nn.sigmoid(x)

def _layernorm(x, axis=-1, eps=1e-05):
    m = jnp.mean(x, axis=axis, keepdims=True)
    v = jnp.var(x, axis=axis, keepdims=True)
    return (x - m) / jnp.sqrt(v + eps)

def _scatter_add(tgt, idx, src, axis=0):
    return tgt.at[idx].add(src)

def _segment_sum(src, seg, n):
    return jax.ops.segment_sum(src, seg, n)
kernel_name = 'mk_flamingo_gated_d1_seqx_r4_760823'

def setup_inputs(seed: int=0):
    np.random.seed(seed)
    _w = jnp.asarray

    def _rec_inputs():
        import jax
        import jax.numpy as jnp
        _rk = jax.random.key(seed)
        x = -0.0002928 + 1 * jax.random.normal(jax.random.fold_in(_rk, 1), (64, 256, 256), jnp.float32)
        _lenS = 256 - jax.random.randint(jax.random.fold_in(_rk, 7), (64,), 0, max(1, 256 // 4) + 1, jnp.int32)
        _lenS2 = 77 - jax.random.randint(jax.random.fold_in(_rk, 8), (64,), 0, max(1, 77 // 4) + 1, jnp.int32)
        _ctx_1024P = jax.random.normal(jax.random.fold_in(_rk, 11), (64, 16, 256), jnp.float32)
        _ctx_1024c = jax.random.dirichlet(jax.random.fold_in(_rk, 511), 0.3 * jnp.ones((16,), jnp.float32), (64, 77))
        _ctx_1024t = jnp.einsum('bsk,bkd->bsd', _ctx_1024c, _ctx_1024P)
        _ctx_1024t = _ctx_1024t * jax.lax.rsqrt(jnp.mean(jnp.square(_ctx_1024t)) + 1e-12) * 0.953939
        ctx_1024 = -1.39393e-06 + 0.999914 * (_ctx_1024t + 0.3 * jax.random.normal(jax.random.fold_in(_rk, 611), (64, 77, 256), jnp.float32))
        _g = jax.random.normal(jax.random.fold_in(_rk, 9001), (2, 1), jnp.float32)
        _g = jnp.sign(_g) * jnp.maximum(jnp.abs(_g), 1.0) + (_g == 0) * 1.0
        g_xattn = _g[0]
        g_ffn = _g[1]
        return (x, ctx_1024, g_xattn, g_ffn)
    x, ctx_1024, g_xattn, g_ffn = _rec_inputs()

    def _L0_xattn_setup():
        import jax, jax.numpy as jnp
        import numpy as np
        DIM = 256
        HEAD_DIM = 64
        NUM_HEADS = DIM // HEAD_DIM
        EPS = 1e-05

        def rms_norm(x, w):
            xf = x.astype(jnp.float32)
            n = xf * jax.lax.rsqrt(jnp.mean(xf * xf, axis=-1, keepdims=True) + EPS)
            return n.astype(x.dtype) * w.astype(x.dtype)
        key = jax.random.key(seed)
        ks = jax.random.split(key, 8)
        s = 1.0 / np.sqrt(DIM)
        return {'q_input': jax.random.normal(ks[0], (2, 512, DIM), dtype=jnp.float32), 'kv_input': jax.random.normal(ks[1], (2, 512, DIM), dtype=jnp.float32), 'Wq': jax.random.normal(ks[2], (DIM, DIM), dtype=jnp.float32) * s, 'Wkv': jax.random.normal(ks[3], (DIM, 2 * DIM), dtype=jnp.float32) * s, 'Wfc': jax.random.normal(ks[4], (DIM, DIM), dtype=jnp.float32) * s, 'fc_b': jnp.zeros((DIM,), dtype=jnp.float32), 'qn_w': jnp.ones((HEAD_DIM,), dtype=jnp.float32), 'kn_w': jnp.ones((HEAD_DIM,), dtype=jnp.float32)}
    _L0_xattn_all = _L0_xattn_setup()
    _L0_xattn_in = {k: v for k, v in _L0_xattn_all.items() if k in ('Wq', 'Wkv', 'Wfc', 'fc_b', 'qn_w', 'kn_w')}
    del _L0_xattn_all

    def _L0_ffn_setup():
        import jax, jax.numpy as jnp
        import numpy as np
        B, T, D, E, TOP_K = (4, 1024, 256, 8, 2)
        CAPACITY_FACTOR = 1.5
        key = jax.random.key(seed)
        k1, k2, k3 = jax.random.split(key, 3)
        x = jax.random.normal(k1, (B, T, D), dtype=jnp.float32)
        Wr = jax.random.normal(k2, (E, D), dtype=jnp.float32) * 0.02
        We = jax.random.normal(k3, (E, D, D), dtype=jnp.float32) * 0.02
        return {'x': x, 'Wr': Wr, 'We': We}
    _L0_ffn_all = _L0_ffn_setup()
    _L0_ffn_in = {k: v for k, v in _L0_ffn_all.items() if k in ('Wr', 'We')}
    del _L0_ffn_all
    return {'x': x, 'ctx_1024': ctx_1024, 'g_xattn': g_xattn, 'g_ffn': g_ffn, 'L0_xattn_Wq': _L0_xattn_in['Wq'], 'L0_xattn_Wkv': _L0_xattn_in['Wkv'], 'L0_xattn_Wfc': _L0_xattn_in['Wfc'], 'L0_xattn_fc_b': _L0_xattn_in['fc_b'], 'L0_xattn_qn_w': _L0_xattn_in['qn_w'], 'L0_xattn_kn_w': _L0_xattn_in['kn_w'], 'L0_ffn_Wr': _L0_ffn_in['Wr'], 'L0_ffn_We': _L0_ffn_in['We']}

def reference(x, ctx_1024, g_xattn, g_ffn, L0_xattn_Wq, L0_xattn_Wkv, L0_xattn_Wfc, L0_xattn_fc_b, L0_xattn_qn_w, L0_xattn_kn_w, L0_ffn_Wr, L0_ffn_We):
    import jax
    import jax.numpy as jnp

    def _L0_xattn_ref(q_input, kv_input, Wq, Wkv, Wfc, fc_b, qn_w, kn_w):
        import jax, jax.numpy as jnp
        import numpy as np
        DIM = 256
        HEAD_DIM = 64
        NUM_HEADS = DIM // HEAD_DIM
        EPS = 1e-05

        def rms_norm(x, w):
            xf = x.astype(jnp.float32)
            n = xf * jax.lax.rsqrt(jnp.mean(xf * xf, axis=-1, keepdims=True) + EPS)
            return n.astype(x.dtype) * w.astype(x.dtype)
        b, lq, _ = q_input.shape
        lk = kv_input.shape[1]
        q = (q_input @ Wq).reshape(b, lq, NUM_HEADS, HEAD_DIM)
        kv = kv_input @ Wkv
        k, v = jnp.split(kv, 2, axis=-1)
        k = k.reshape(b, lk, NUM_HEADS, HEAD_DIM)
        v = v.reshape(b, lk, NUM_HEADS, HEAD_DIM)
        q = rms_norm(q, qn_w)
        k = rms_norm(k, kn_w)
        scale = 1.0 / np.sqrt(HEAD_DIM)
        scores = jnp.einsum('bqhd,bkhd->bhqk', q, k) * scale
        attn = jax.nn.softmax(scores, axis=-1)
        x = jnp.einsum('bhqk,bkhd->bqhd', attn, v)
        x = x.reshape(b, lq, DIM)
        return x @ Wfc + fc_b

    def _L0_ffn_ref(x, Wr, We):
        import jax, jax.numpy as jnp
        import numpy as np
        B, T, D, E, TOP_K = (4, 1024, 256, 8, 2)
        CAPACITY_FACTOR = 1.5
        Bb, Tt, Dd = x.shape
        Ee = Wr.shape[0]
        K = TOP_K
        C = int(Tt * K / Ee * CAPACITY_FACTOR) + 1
        logits = jnp.einsum('btd,ed->bte', x, Wr)
        top_vals, top_idx = jax.lax.top_k(logits, K)
        w = jax.nn.softmax(top_vals, axis=-1)
        flat_e = top_idx.reshape(Bb, Tt * K)
        oh = jax.nn.one_hot(flat_e, Ee, dtype=jnp.int32)
        pos_all = jnp.cumsum(oh, axis=1) - oh
        pos = jnp.take_along_axis(pos_all, flat_e[..., None], axis=-1)[..., 0]
        keep = pos < C
        b_idx = jnp.arange(Bb, dtype=jnp.int32)[:, None]
        dst = (b_idx * Ee + flat_e) * C + pos
        dst = jnp.where(keep, dst, Bb * Ee * C).reshape(-1)
        x_rep = jnp.repeat(x, K, axis=1).reshape(-1, Dd)
        buf = jnp.zeros((Bb * Ee * C, Dd), dtype=x.dtype).at[dst].add(x_rep, mode='drop')
        expert_in = buf.reshape(Bb, Ee, C, Dd)
        expert_out = jnp.einsum('becd,edf->becf', expert_in, We)
        gathered = jnp.take(expert_out.reshape(Bb * Ee * C, Dd), dst, axis=0, mode='fill', fill_value=0.0)
        gathered = gathered.reshape(Bb, Tt, K, Dd)
        out = jnp.einsum('btk,btkd->btd', w, gathered)
        return out
    x = x + jnp.tanh(g_xattn[0]) * _L0_xattn_ref(_layernorm(x, axis=-1), ctx_1024, L0_xattn_Wq, L0_xattn_Wkv, L0_xattn_Wfc, L0_xattn_fc_b, L0_xattn_qn_w, L0_xattn_kn_w)
    x = x + jnp.tanh(g_ffn[0]) * _L0_ffn_ref(_layernorm(x, axis=-1), L0_ffn_Wr, L0_ffn_We)
    return x

_drawn_inputs = setup_inputs


def setup_inputs(seed=0):
    import zlib

    import numpy as np

    out = dict(_drawn_inputs(seed))
    spreads = {'L0_xattn_fc_b': (0.0, 0.1), 'L0_xattn_qn_w': (1.0, 0.2), 'L0_xattn_kn_w': (1.0, 0.2)}
    factors = {}
    for name, (base, spread) in spreads.items():
        noise = np.random.default_rng([zlib.crc32(name.encode()), seed]).standard_normal(out[name].shape)
        drawn = base * np.exp(spread * noise) if base else spread * noise
        out[name] = jnp.asarray(drawn.astype(out[name].dtype))
    for name, factor in factors.items():
        out[name] = (out[name] * factor).astype(out[name].dtype)
    return out
```

```python
from contextlib import ExitStack

import concourse.bass as bass
from concourse import mybir

F32 = mybir.dt.float32
F32R = mybir.dt.float32r
BF16 = mybir.dt.bfloat16
ALU = mybir.AluOpType
ACT = mybir.ActivationFunctionType
AX = mybir.AxisListType

P = 128
B, LQ, D = 64, 256, 256
LK = 77
H, DH = 4, 64
E, TOPK = 8, 2
CAP = int(LQ * TOPK / E * 1.5) + 1
EPS = 1e-5
KC = D // P
BP = 2
PAIRS = B // BP
SUB = LQ // P
T = BP * SUB
TOK = T * P
HK = H * LK
SPLIT_TERMS = ((0, 0), (0, 1), (1, 0))
BIG = 3.0e38


class Pair:

    def __init__(self, j, c):
        self.n = 2 * j + c
        self.half = j + c // 2
        self.parity = c % 2


class Signal:

    def __init__(self, sem, per_pair, unit=1):
        self.sem, self.per_pair, self.unit = sem, per_pair, unit

    def at(self, pair, k=None):
        return (pair.n * self.per_pair + (self.per_pair if k is None else k)) * self.unit

    def before(self, pair, back=1):
        n = pair.n - (back - 1)
        if isinstance(n, int):
            n = max(n, 0)
        return n * (self.per_pair * self.unit)


def build(nc, x, ctx_in, g_xattn, g_ffn, Wq, Wkv, Wfc, fc_b, qn_w, kn_w, Wr, We, out):
    es = ExitStack()
    with es:
        def sb(name, shape, dt=F32):
            return es.enter_context(nc.sbuf_tensor(name, shape, dt))

        def bank(name):
            return es.enter_context(nc.psum_tensor(name, [P, 512], F32))

        def sem(name):
            return es.enter_context(nc.semaphore(name))

        def sig(name, per_pair, unit=1):
            return Signal(sem(name), per_pair, unit)

        x_v = x.rearrange("(n b) (q s) d -> n q b (s d)", b=BP, s=SUB)
        out_v = out.rearrange("(n b) (q s) d -> n q b (s d)", b=BP, s=SUB)
        ctx_v = ctx_in.rearrange("(n b) k d -> n k b d", b=BP)

        ident = sb("ident", [P, P])
        head_ones = sb("head_ones", [P, 2])
        before = sb("before", [P, P], BF16)
        upto = sb("upto", [P, P], BF16)
        first_weight = sb("first_weight", [P, E])
        minus_half = sb("minus_half", [P, 2 * 8])
        tanh_g = sb("tanh_g", [P, 2])
        bias_bc = sb("bias_bc", [P, D])
        bias_g = sb("bias_g", [P, D])
        qk_w = sb("qk_w", [P, 3])
        stage = sb("stage", [P, 2, E * D])
        stage_r = sb("stage_r", [P, KC, E])
        wq = sb("wq", [P, 2, KC, D], F32R)
        wkv = sb("wkv", [P, 2, KC, 2 * D], F32R)
        wfc = sb("wfc", [P, 2, KC, D], F32R)
        wr = sb("wr", [P, KC, 2, E], F32R)
        we = sb("we", [P, 2, KC, E * D], F32R)

        x_sb = sb("x_sb", [P, 2, T, D])
        ctx_sb = sb("ctx_sb", [LK, 2, BP, D])
        stats1 = sb("stats1", [P, T, 6])
        mv1 = sb("mv1", [P, T, 2])
        ve1 = sb("ve1", [P, T])
        rstd1 = sb("rstd1", [P, T])
        shift1 = sb("shift1", [P, T])
        xn1 = sb("xn1", [P, T, D])
        xb = sb("xb", [P, T, D])
        xT = sb("xT", [P, 2, KC, TOK], F32R)
        cT = sb("cT", [P, 2, KC, BP * LK], F32R)
        k_sq = sb("k_sq", [LK, BP, D])
        k_ss = sb("k_ss", [LK, BP * H])
        k_ve = sb("k_ve", [LK, BP * H])
        k_r = sb("k_r", [LK, BP * H])
        kn = sb("kn", [LK, BP, D])
        kd = sb("kd", [P, 2, BP, KC, 2, LK], F32R)
        vz = sb("vz", [LK, 2, BP, KC, 2 * P], F32R)
        qT = sb("qT", [P, 2, KC, TOK], F32R)
        q_sq = sb("q_sq", [P, KC, TOK])
        q_ve = sb("q_ve", [P, T * H])
        q_r = sb("q_r", [P, T, H])
        s_max = sb("s_max", [P, T, H])
        s_bias = sb("s_bias", [P, T, H])
        probs = sb("probs", [P, T, HK])
        p_sum = sb("p_sum", [P, T, H])
        p_inv = sb("p_inv", [P, T, H])
        pT = sb("pT", [LK, 2, BP, H, SUB, P], F32R)
        oT = sb("oT", [P, 2, KC, TOK], F32R)
        x1 = sb("x1", [P, 2, T, D])
        stats2 = sb("stats2", [P, T, 6])
        mv2 = sb("mv2", [P, T, 2])
        ve2 = sb("ve2", [P, T])
        rstd2 = sb("rstd2", [P, T])
        shift2 = sb("shift2", [P, T])
        xn2 = sb("xn2", [P, T, D])
        x2T = sb("x2T", [P, 2, 2, KC, TOK], F32R)
        lg = sb("lg", [P, T, E])
        lg_lo = sb("lg_lo", [P, T, E])
        lg2 = sb("lg2", [P, T, E])
        eq = sb("eq", [P, T, E])
        rank = sb("rank", [P, T, E])
        first = sb("first", [P, T])
        top = sb("top", [P, 2, T])
        mask = sb("mask", [P, 2, T, E])
        both = sb("both", [P, T, E], BF16)
        gap = sb("gap", [P, T])
        egap = sb("egap", [P, T])
        den = sb("den", [P, T])
        w_top = sb("w_top", [P, 2, T])
        g_part = sb("g_part", [P, 2, T, E])
        g_all = sb("g_all", [P, T, E])
        gate = sb("gate", [P, 2, T, E])
        acc_v = sb("acc_v", [P, T, D])
        a_out = sb("a_out", [P, 2, E // 2, D])
        a_sum = sb("a_sum", [P, 2, D])
        y = sb("y", [P, T, D])

        bkA, bkB, bkC, bkD, bkE, bkF = (bank(f"bk{c}") for c in "ABCDEF")
        bkM = [bank("bkM0"), bank("bkM1")]
        cT_psum = bkE[:, 0:KC * BP * LK]
        kT_psum = bkD[:, 0:BP * KC * LK].rearrange("p (b m k) -> p b m k", b=BP, m=KC)
        ssq_ps = bkE[:, 0:T * H]
        lg_ps = bkC[:, 0:T * 2 * E].rearrange("p (t a e) -> p t a e", a=2, e=E)
        pos_ps = bkC[:, T * 2 * E:T * 3 * E]
        xT_bank = [bkA, bkB]
        q_bank = [bkA, bkB]
        kv_bank = [bkD, bkE]
        s_bank = [bkA, bkB, bkD, bkE]
        o_bank = [bkF, bkC]
        fc_bank = [bkA, bkB]
        x2T_bank = [bkF, bkC]

        w_in = sem("w_in")
        stage_in = [sem(f"stage_in{n}") for n in range(6)]
        stage_used = sem("stage_used")
        const_ready = sem("const_ready")
        tanh_ready = sem("tanh_ready")
        hi_ready = sem("hi_ready")
        setup_v = sem("setup_v")
        waits_alone = sem("waits_alone")
        x_in = [sem("x_in0"), sem("x_in1")]
        ctx_sem = [sem("ctx_in0"), sem("ctx_in1")]
        y_out = [sig("y_out0", 1, 16), sig("y_out1", 1, 16)]
        stats1_done = sig("stats1_done", 4)
        var1_done = sig("var1_done", 5)
        rstd1_done = sig("rstd1_done", 1)
        shift1_done = sig("shift1_done", 1)
        xn1_done = sig("xn1_done", T)
        xb_done = sig("xb_done", T)
        xT_ps = sig("xT_ps", KC)
        xT_hi = sig("xT_hi", KC)
        xT_lo = sig("xT_lo", KC)
        cT_ps = sig("cT_ps", 1)
        cT_hi = sig("cT_hi", 1)
        cT_lo = sig("cT_lo", 1)
        kv_ps = sig("kv_ps", BP)
        k_sq_done = sig("k_sq_done", BP)
        v_hi = sig("v_hi", BP)
        v_lo = sig("v_lo", BP)
        k_ss_done = sig("k_ss_done", BP + 1)
        k_r_done = sig("k_r_done", 1)
        kn_done = sig("kn_done", BP)
        kT_ps = sig("kT_ps", 1)
        k_hi = sig("k_hi", 2)
        k_lo = sig("k_lo", 2)
        q_ps = sig("q_ps", KC)
        q_hi = sig("q_hi", KC)
        q_sq_done = sig("q_sq_done", KC)
        q_lo = sig("q_lo", KC)
        ssq_done = sig("ssq_done", 1)
        q_ve_done = sig("q_ve_done", 1)
        q_r_done = sig("q_r_done", 1)
        s_ps = sig("s_ps", T)
        s_max_done = sig("s_max_done", T)
        s_bias_done = sig("s_bias_done", T)
        exp_done = sig("exp_done", T)
        p_inv_done = sig("p_inv_done", T)
        probs_done = sig("probs_done", T)
        pT_ps = sig("pT_ps", T)
        pT_hi = sig("pT_hi", T)
        pT_lo = sig("pT_lo", T)
        o_ps = sig("o_ps", KC)
        o_hi = sig("o_hi", KC)
        o_lo = sig("o_lo", KC)
        fc_ps = sig("fc_ps", 2)
        x1_done = sig("x1_done", 2)
        stats2_done = sig("stats2_done", T)
        var2_done = sig("var2_done", T + 1)
        rstd2_done = sig("rstd2_done", 1)
        shift2_done = sig("shift2_done", 1)
        xn2_done = sig("xn2_done", T)
        x2T_ps = sig("x2T_ps", KC)
        x2T_hi = sig("x2T_hi", KC)
        x2T_lo = sig("x2T_lo", KC)
        lg_done = sig("lg_done", 1)
        lg_lo_done = sig("lg_lo_done", 1)
        top2 = sig("top2", 14)
        egap_done = sig("egap_done", 1)
        GATE_STEPS = 8
        gate_chain = sig("gate_chain", GATE_STEPS)
        pos_done = sig("pos_done", 1)
        CH = T * E // 2
        moe_ps = sig("moe_ps", CH)
        v_added = sig("v_added", CH)
        a_ready = sig("a_ready", CH // 2)
        a_summed = sig("a_summed", 3 * T)
        y_done = [sig(f"y_done{t}", 1) for t in range(T)]

        def chunked(a, n):
            return a.rearrange("p (k f) -> p k f", f=n)

        weights = [
            (chunked(stage[:, 0, 0:KC * D], D), Wq.rearrange("(k p) f -> p k f", p=P), None, wq),
            (chunked(stage[:, 0, KC * D:3 * KC * D], 2 * D), Wkv.rearrange("(k p) f -> p k f", p=P), None, wkv),
            (chunked(stage[:, 0, 3 * KC * D:4 * KC * D], D), Wfc.rearrange("(k p) f -> p k f", p=P),
             tanh_g[:, 0:1], wfc),
            (stage_r[:], Wr.rearrange("e (k p) -> p k e", p=P), None,
             wr[:].rearrange("p k a e -> p a k e")),
        ] + [(chunked(stage[:, 1 - k], D), We[:, k * P:(k + 1) * P, :].rearrange("e p f -> p e f"),
              tanh_g[:, 1:2], we[:, :, k].rearrange("p a (e f) -> p a e f", f=D)) for k in range(KC)]
        FRONT_WEIGHTS = 4
        STAGE0_USERS = 3

        SLOTS = T * E // 2
        GAP_STEP, ROUTE_STEPS = 9, 14

        def v_heads(b):
            return kv_bank[b][0:LK, D:2 * D].rearrange("k (m j d) -> k m j d", m=KC, j=2)

        def vz_heads(part, b):
            return vz[:, part, b].rearrange("k m (c d) -> k m c d", d=DH)[:, :, 0:4:3, :]

        def product(out, pairs):
            terms = [(l[a], r[b]) for l, r in pairs for a, b in SPLIT_TERMS]
            for i, (l, r) in enumerate(terms):
                mm = nc.tensor.matmul(out, l, r, start=(i == 0), stop=(i == len(terms) - 1))
            return mm

        LOOPS = (PAIRS - 4) // 2

        def tile_before_last(m, t):
            other = y_done[(t + 2) % T]
            return other.before(m) if t < 2 else other.at(m)

        def pipeline(engine, fill, step):
            fill()
            step(Pair(0, 0), Pair(0, 1), Pair(0, 2), Pair(0, 3))
            with engine.Fori(0, LOOPS) as j:
                step(Pair(j, 1), Pair(j, 2), Pair(j, 3), Pair(j, 4))
                step(Pair(j, 2), Pair(j, 3), Pair(j, 4), Pair(j, 5))
            step(Pair(LOOPS, 1), Pair(LOOPS, 2), Pair(LOOPS, 3), None)
            step(Pair(LOOPS, 2), Pair(LOOPS, 3), None, None)
            step(Pair(LOOPS, 3), None, None, None)

        block = es.enter_context(nc.Block())

        @block.sync
        def _(sp):
            with nc.allow_non_contiguous_dma("small one-time loads"):
                for dst, src in ((tanh_g[:, 0:1], g_xattn.partition_broadcast(P)),
                                 (tanh_g[:, 1:2], g_ffn.partition_broadcast(P)),
                                 (bias_bc[:], fc_b.partition_broadcast(P)),
                                 (qk_w[0:DH, 0:1], qn_w.rearrange("(d o) -> d o", o=1)),
                                 (qk_w[DH:P, 0:1], qn_w.rearrange("(d o) -> d o", o=1)),
                                 (qk_w[0:DH, 1:2], kn_w.rearrange("(d o) -> d o", o=1)),
                                 (qk_w[DH:P, 1:2], kn_w.rearrange("(d o) -> d o", o=1))):
                    sp.dma_start(dst, src).then_inc(w_in, 16)

            def load(pair):
                for used in (xb_done, xn1_done, cT_ps):
                    sp.wait_ge(used.sem, used.before(pair, 2))
                    sp.sem_inc(waits_alone, 1)
                sp.dma_start(ctx_sb[:, pair.parity], ctx_v[pair.n]).then_inc(ctx_sem[pair.parity], 16)
                sp.dma_start(x_sb[:, pair.parity].rearrange("p (b s) d -> p b (s d)", b=BP),
                             x_v[pair.n]).then_inc(x_in[pair.parity], 16)

            load(Pair(0, 0))
            load(Pair(0, 1))
            with nc.allow_non_contiguous_dma("router weights, once"):
                for n, (view, src, _, _) in enumerate(weights):
                    if n == len(weights) - 1:
                        sp.wait_ge(stage_used, STAGE0_USERS)
                    if src.shape[-1] == E:
                        for k in range(KC):
                            sp.dma_start(view[:, k], src[:, k]).then_inc(stage_in[n], 16)
                    else:
                        sp.dma_start(view, src).then_inc(stage_in[n], 16)

            def store(pair, b):
                for t in range(b * SUB, (b + 1) * SUB):
                    sp.wait_ge(y_done[t].sem, y_done[t].at(pair))
                    sp.sem_inc(waits_alone, 1)
                sp.dma_start(out_v[pair.n][:, b], y[:, b * SUB:(b + 1) * SUB].rearrange("p s d -> p (s d)")
                             ).then_inc(y_out[b].sem, 16)

            def step(m, p, f, ahead):
                if ahead:
                    load(ahead)
                store(m, 0)
                store(m, 1)

            pipeline(sp, lambda: load(Pair(0, 2)), step)
            for b in range(BP):
                sp.wait_ge(y_out[b].sem, 16 * PAIRS)

        @block.gpsimd
        def _(pool):
            pool.memset(ident[:], 0.0).then_inc(const_ready, 1)
            pool.memset(before[:], 1.0).then_inc(const_ready, 1)
            pool.memset(upto[:], 1.0).then_inc(const_ready, 1)
            pool.memset(minus_half[:], -0.5).then_inc(const_ready, 1)
            for e in range(E):
                pool.memset(first_weight[:, e:e + 1], float(E - e)).then_inc(const_ready, 1)
            pool.wait_ge(const_ready, 4 + E)
            pool.affine_select(out=ident[:], in_=ident[:], compare_op=ALU.not_equal, fill=1.0, base=0,
                               pattern=[[-1, P]], channel_multiplier=1).then_inc(const_ready, 1)
            pool.affine_select(out=before[:], in_=before[:], compare_op=ALU.is_gt, fill=0.0, base=0,
                               pattern=[[1, P]], channel_multiplier=-1).then_inc(const_ready, 1)
            pool.affine_select(out=upto[:], in_=upto[:], compare_op=ALU.is_ge, fill=0.0, base=0,
                               pattern=[[1, P]], channel_multiplier=-1).then_inc(const_ready, 1)

            def pow_m_half(dst, src, n, parts):
                return nc.gpsimd.tensor_tensor(dst, src, minus_half[0:parts, 0:n], ALU.pow)

            def ln1(f):
                pool.wait_ge(var1_done.sem, var1_done.at(f))
                pool.wait_ge(xn1_done.sem, xn1_done.before(f))
                pow_m_half(rstd1[:], ve1[:], T, P).then_inc(rstd1_done.sem, 1)

            def make_xb(f, t):
                pool.wait_ge(x1_done.sem, x1_done.before(f))
                nc.gpsimd.tensor_tensor(xb[:, t], x_sb[:, f.parity, t], bias_g[:], ALU.add
                                        ).then_inc(xb_done.sem, 1)

            def ln2(p):
                pool.wait_ge(var2_done.sem, var2_done.at(p))
                pool.wait_ge(xn2_done.sem, xn2_done.before(p))
                pow_m_half(rstd2[:], ve2[:], T, P).then_inc(rstd2_done.sem, 1)

            def k_rsqrt(f):
                pool.wait_ge(k_ss_done.sem, k_ss_done.at(f))
                pow_m_half(k_r[:], k_ve[:], BP * H, LK).then_inc(k_r_done.sem, 1)

            def q_rsqrt(f):
                pool.wait_ge(q_ve_done.sem, q_ve_done.at(f))
                pow_m_half(q_r[:].rearrange("p t h -> p (t h)"), q_ve[:], T * H, P
                           ).then_inc(q_r_done.sem, 1)

            def normalise(f, t):
                pool.wait_ge(p_inv_done.sem, p_inv_done.at(f, t + 1))
                pr = probs[:, t].rearrange("p (h k) -> p h k", k=LK)
                nc.gpsimd.tensor_tensor(pr, pr, p_inv[:, t].unsqueeze(2).to_broadcast([P, H, LK]), ALU.mult
                                        ).then_inc(probs_done.sem, 1)

            def finish_tile(m, t):
                o, a = a_out[:, t % 2], a_sum[:, t % 2]
                for i in range(1, 4):
                    if i == 1:
                        pool.wait_ge(a_ready.sem, a_ready.at(m, 2 * t + 1))
                        pool.wait_ge(y_done[(t + 2) % T].sem, tile_before_last(m, t))
                    else:
                        pool.wait_ge(a_ready.sem, a_ready.at(m, 2 * t + 2))
                        pool.wait_ge(a_summed.sem, a_summed.at(m, 3 * t + i - 1))
                    nc.gpsimd.tensor_tensor(a, o[:, 0] if i == 1 else a, o[:, i], ALU.add
                                            ).then_inc(a_summed.sem, 1)
                pool.wait_ge(v_added.sem, v_added.at(m, 4 * (t + 1)))
                pool.wait_ge(a_summed.sem, a_summed.at(m, 3 * t + 3))
                pool.wait_ge(y_out[t // SUB].sem, y_out[t // SUB].before(m))
                nc.gpsimd.tensor_tensor(y[:, t], a, acc_v[:, t], ALU.add).then_inc(y_done[t].sem, 1)

            pool.wait_ge(setup_v, 2)
            def slots(m, p, f):
                if f:
                    ln1(f)
                if p:
                    ln2(p)
                if f:
                    k_rsqrt(f)
                if m:
                    finish_tile(m, 0)
                if f:
                    make_xb(f, 0)
                    make_xb(f, 1)
                    q_rsqrt(f)
                if m:
                    finish_tile(m, 1)
                if f:
                    make_xb(f, 2)
                    make_xb(f, 3)
                    for t in range(T):
                        normalise(f, t)
                if m:
                    finish_tile(m, 2)
                    finish_tile(m, 3)

            def fill():
                slots(None, None, Pair(0, 0))
                slots(None, Pair(0, 0), Pair(0, 1))

            def step(m, p, f, ahead):
                slots(m, p, f)

            pipeline(pool, fill, step)

        @block.scalar
        def _(act):
            act.wait_ge(w_in, 16 * 7)
            nc.scalar.activation(tanh_g[:], tanh_g[:], ACT.Tanh).then_inc(tanh_ready, 1)
            act.wait_ge(tanh_ready, 1)
            for n, (view, src, scale, w) in enumerate(weights):
                act.wait_ge(stage_in[n], 16 * (KC if src.shape[-1] == E else 1))
                if scale is None:
                    nc.scalar.activation(w[:, 0], view, ACT.Copy).then_inc(hi_ready, 1)
                else:
                    nc.scalar.activation(w[:, 0], view, ACT.Copy, scale=scale).then_inc(hi_ready, 1)

            def copy(dst, src, **kw):
                return nc.scalar.activation(dst, src, ACT.Copy, **kw)

            def ln1(f):
                act.wait_ge(shift1_done.sem, shift1_done.at(f))
                act.wait_ge(xT_ps.sem, xT_ps.before(f))
                for t in range(T):
                    nc.scalar.activation(xn1[:, t], x_sb[:, f.parity, t], ACT.Identity,
                                         scale=rstd1[:, t:t + 1], bias=shift1[:, t:t + 1]
                                         ).then_inc(xn1_done.sem, 1)

            def ln2(p):
                act.wait_ge(shift2_done.sem, shift2_done.at(p))
                act.wait_ge(x2T_ps.sem, x2T_ps.before(p))
                for t in range(T):
                    nc.scalar.activation(xn2[:, t], x1[:, p.parity, t], ACT.Identity,
                                         scale=rstd2[:, t:t + 1], bias=shift2[:, t:t + 1]
                                         ).then_inc(xn2_done.sem, 1)

            def ctx_hi(f):
                act.wait_ge(cT_ps.sem, cT_ps.at(f))
                act.wait_ge(kv_ps.sem, kv_ps.before(f))
                copy(cT[:, 0], cT_psum.rearrange("p (k c) -> p k c", k=KC)).then_inc(cT_hi.sem, 1)

            def xT_part(f, k):
                act.wait_ge(xT_ps.sem, xT_ps.at(f, k + 1))
                act.wait_ge(q_ps.sem, q_ps.before(f))
                copy(xT[:, 0, k], xT_bank[k][:]).then_inc(xT_hi.sem, 1)

            def kv(f, b):
                act.wait_ge(kv_ps.sem, kv_ps.at(f, b + 1))
                act.wait_ge(k_ss_done.sem, k_ss_done.before(f))
                nc.scalar.activation(k_sq[:, b], kv_bank[b][0:LK, 0:D], ACT.Square
                                     ).then_inc(k_sq_done.sem, 1)
                act.wait_ge(o_ps.sem, o_ps.before(f))
                copy(vz_heads(0, b), v_heads(b)).then_inc(v_hi.sem, 1)

            def q(f, m):
                act.wait_ge(q_ps.sem, q_ps.at(f, m + 1))
                act.wait_ge(ssq_done.sem, ssq_done.before(f))
                nc.scalar.activation(q_sq[:, m], q_bank[m][:], ACT.Square).then_inc(q_sq_done.sem, 1)
                act.wait_ge(s_ps.sem, s_ps.before(f))
                copy(qT[:, 0, m], q_bank[m][:]).then_inc(q_hi.sem, 1)

            def k_part(f):
                act.wait_ge(kT_ps.sem, kT_ps.at(f))
                act.wait_ge(s_ps.sem, s_ps.before(f))
                for j in range(2):
                    h = slice(j * DH, (j + 1) * DH)
                    copy(kd[h, 0, :, :, j], kT_psum[h], scale=qk_w[h, 2:3]).then_inc(k_hi.sem, 1)

            def exps(f, t):
                act.wait_ge(s_bias_done.sem, s_bias_done.at(f, t + 1))
                if t == 0:
                    act.wait_ge(pT_ps.sem, pT_ps.before(f))
                for h in range(H):
                    ins = nc.scalar.activation(probs[:, t, h * LK:(h + 1) * LK],
                                               s_bank[t][:, h * LK:(h + 1) * LK], ACT.Exp,
                                               scale=q_r[:, t, h:h + 1], bias=s_bias[:, t, h:h + 1],
                                               accum_out=p_sum[:, t, h:h + 1])
                ins.then_inc(exp_done.sem, 1)

            def pT_part(f, t):
                act.wait_ge(pT_ps.sem, pT_ps.at(f, t + 1))
                act.wait_ge(o_ps.sem, o_ps.before(f))
                copy(pT[:, 0, t // SUB, :, t % SUB], s_bank[t][0:LK, :].rearrange("k (h q) -> k h q", h=H)
                     ).then_inc(pT_hi.sem, 1)

            def o_part(f, m):
                act.wait_ge(o_ps.sem, o_ps.at(f, m + 1))
                act.wait_ge(fc_ps.sem, fc_ps.before(f))
                copy(oT[:, 0, m], o_bank[m][:]).then_inc(o_hi.sem, 1)

            def x2T_part(p, k):
                act.wait_ge(x2T_ps.sem, x2T_ps.at(p, k + 1))
                act.wait_ge(moe_ps.sem, moe_ps.before(p, 2))
                act.wait_ge(lg_done.sem, lg_done.before(p, 2))
                copy(x2T[:, p.parity, 0, k], x2T_bank[k][:]).then_inc(x2T_hi.sem, 1)

            def router_exp(p):
                act.wait_ge(top2.sem, top2.at(p, GAP_STEP))
                act.wait_ge(gate_chain.sem, gate_chain.before(p))
                nc.scalar.activation(egap[:], gap[:], ACT.Exp).then_inc(egap_done.sem, 1)

            def experts(m, c):
                t = c // (E // 2)
                act.wait_ge(moe_ps.sem, moe_ps.at(m, c + 1))
                act.wait_ge(gate_chain.sem, gate_chain.at(m))
                act.wait_ge(y_done[(t + 2) % T].sem, tile_before_last(m, t))
                for i in range(2):
                    e = 2 * (c % (E // 2)) + i
                    ins = nc.scalar.activation(a_out[:, t % 2, (e // 4) * 2 + i],
                                               bkM[1][:, i * D:(i + 1) * D], ACT.Copy,
                                               scale=gate[:, m.parity, t, e:e + 1])
                ins.then_inc(a_ready.sem, 1)

            def slot(k, m, p, f):
                if k == 0 and p:
                    o_part(p, 1)
                if k == 1 and f:
                    ctx_hi(f)
                if k == 2 and f:
                    ln1(f)
                if k == 3 and f:
                    kv(f, 0)
                if k == 4 and f:
                    xT_part(f, 0)
                    xT_part(f, 1)
                    kv(f, 1)
                if k == 5 and p:
                    ln2(p)
                if k == 6 and f:
                    q(f, 0)
                if k == 7 and f:
                    q(f, 1)
                if k == 7 and p:
                    x2T_part(p, 0)
                    x2T_part(p, 1)
                if k == 8 and f:
                    k_part(f)
                if k == 9 and f:
                    exps(f, 0)
                if k == 10 and f:
                    exps(f, 1)
                    exps(f, 2)
                if k == 11 and f:
                    exps(f, 3)
                if k == 13 and f:
                    pT_part(f, 0)
                    pT_part(f, 1)
                if k == 13 and p:
                    router_exp(p)
                if k == 14 and f:
                    pT_part(f, 2)
                    pT_part(f, 3)
                if k == 15 and f:
                    o_part(f, 0)
                if m and k % 2:
                    experts(m, k)

            def fill():
                for f, p in ((Pair(0, 0), None), (Pair(0, 1), Pair(0, 0))):
                    for k in range(SLOTS):
                        slot(k, None, p, f)

            def step(m, p, f, ahead):
                for k in range(SLOTS):
                    slot(k, m, p, f)

            pipeline(act, fill, step)

        @block.vector
        def _(dve):
            dve.memset(kd[:].bitcast(F32).rearrange("p a b c d e -> p (a b c d e)"), 0.0).then_inc(setup_v, 1)
            dve.wait_ge(tanh_ready, 1)
            nc.vector.tensor_scalar(bias_g[:], bias_bc[:], tanh_g[:, 0:1], None, ALU.mult).then_inc(setup_v, 1)
            dve.memset(vz[:].bitcast(F32).rearrange("p a b c d -> p (a b c d)"), 0.0).then_inc(setup_v, 1)
            nc.vector.scalar_tensor_tensor(out=qk_w[:, 2:3], in0=qk_w[:, 0:1], scalar=float(DH) ** -0.5,
                                           in1=qk_w[:, 1:2], op0=ALU.mult, op1=ALU.mult).then_inc(setup_v, 1)
            dve.memset(head_ones[:], 0.0).then_inc(setup_v, 1)
            dve.wait_ge(setup_v, 5)
            for j in range(2):
                dve.memset(head_ones[j * DH:(j + 1) * DH, j:j + 1], 1.0).then_inc(setup_v, 1)
            for n, (view, _, scale, w) in enumerate(weights):
                dve.wait_ge(hi_ready, n + 1)
                if scale is None:
                    nc.vector.tensor_tensor(w[:, 1], view, w[:, 0].bitcast(F32), ALU.subtract
                                            ).then_inc(stage_used, 1)
                else:
                    nc.vector.scalar_tensor_tensor(out=w[:, 1], in0=view, scalar=scale,
                                                   in1=w[:, 0].bitcast(F32), op0=ALU.mult,
                                                   op1=ALU.subtract).then_inc(stage_used, 1)

            def lo(dst, src, hi):
                return nc.vector.tensor_tensor(dst, src, hi.bitcast(F32), ALU.subtract)

            def layernorm_stats(pair, src, stats, mv, ve, stats_done, var_done, tiles):
                for t in tiles:
                    nc.vector.bn_stats(stats[:, t], src[:, t]).then_inc(stats_done.sem, 1)
                for t in tiles:
                    dve.wait_ge(stats_done.sem, stats_done.at(pair, t + 1))
                    dve.sem_inc(waits_alone, 1)
                    nc.vector.bn_aggr(mv[:, t], stats[:, t]).then_inc(var_done.sem, 1)
                if tiles[-1] == T - 1:
                    dve.wait_ge(var_done.sem, var_done.at(pair, T))
                    nc.vector.tensor_scalar(ve[:], mv[:, :, 1], EPS, None, ALU.add).then_inc(var_done.sem, 1)

            def ln1(f):
                dve.wait_ge(x_in[f.parity], 16 * f.half + 16)
                dve.wait_ge(xn1_done.sem, xn1_done.before(f))
                layernorm_stats(f, x_sb[:, f.parity], stats1, mv1, ve1, stats1_done, var1_done, range(T))

            def shift(mv, rstd, dst):
                return nc.vector.scalar_tensor_tensor(out=dst, in0=mv[:, :, 0], scalar=-1.0, in1=rstd[:],
                                                      op0=ALU.mult, op1=ALU.mult)

            def ln1_shift(f):
                dve.wait_ge(rstd1_done.sem, rstd1_done.at(f))
                shift(mv1, rstd1, shift1[:]).then_inc(shift1_done.sem, 1)

            def ln2_shift(p):
                dve.wait_ge(rstd2_done.sem, rstd2_done.at(p))
                shift(mv2, rstd2, shift2[:]).then_inc(shift2_done.sem, 1)

            def residual(p, i):
                dve.wait_ge(fc_ps.sem, fc_ps.at(p, i + 1))
                dve.wait_ge(xb_done.sem, xb_done.at(p))
                if i == 0:
                    dve.wait_ge(xn2_done.sem, xn2_done.before(p))
                dve.wait_ge(v_added.sem, v_added.before(p, 2))
                ts = slice(2 * i, 2 * i + 2)
                nc.vector.tensor_tensor(x1[:, p.parity, ts], fc_bank[i][:].rearrange("p (t d) -> p t d", d=D),
                                        xb[:, ts], ALU.add).then_inc(x1_done.sem, 1)
                dve.wait_ge(x1_done.sem, x1_done.at(p, i + 1))
                layernorm_stats(p, x1[:, p.parity], stats2, mv2, ve2, stats2_done, var2_done,
                                range(2 * i, 2 * i + 2))

            def ctx_lo(f):
                dve.wait_ge(cT_hi.sem, cT_hi.at(f))
                lo(cT[:, 1], cT_psum.rearrange("p (k c) -> p k c", k=KC), cT[:, 0]).then_inc(cT_lo.sem, 1)

            def xT_part(f, k):
                dve.wait_ge(xT_hi.sem, xT_hi.at(f, k + 1))
                lo(xT[:, 1, k], xT_bank[k][:], xT[:, 0, k]).then_inc(xT_lo.sem, 1)

            def kv(f, b):
                dve.wait_ge(k_sq_done.sem, k_sq_done.at(f, b + 1))
                nc.vector.tensor_reduce(k_ss[:, b * H:(b + 1) * H], k_sq[:, b].rearrange("k (h d) -> k h d", d=DH),
                                        AX.X, ALU.add).then_inc(k_ss_done.sem, 1)
                dve.wait_ge(v_hi.sem, v_hi.at(f, b + 1))
                lo(vz_heads(1, b), v_heads(b), vz_heads(0, b)).then_inc(v_lo.sem, 1)
                if b == BP - 1:
                    dve.wait_ge(k_ss_done.sem, k_ss_done.at(f, BP))
                    nc.vector.tensor_scalar(k_ve[:], k_ss[:], 1.0 / DH, EPS, ALU.mult, ALU.add
                                            ).then_inc(k_ss_done.sem, 1)

            def k_scale(f):
                dve.wait_ge(k_r_done.sem, k_r_done.at(f))
                for b in range(BP):
                    nc.vector.tensor_tensor(
                        kn[:, b].rearrange("k (h d) -> k h d", d=DH),
                        kv_bank[b][0:LK, 0:D].rearrange("k (h d) -> k h d", d=DH),
                        k_r[:, b * H:(b + 1) * H].unsqueeze(2).to_broadcast([LK, H, DH]), ALU.mult
                    ).then_inc(kn_done.sem, 1)

            def k_part(f):
                for j in range(2):
                    dve.wait_ge(k_hi.sem, k_hi.at(f, j + 1))
                    h = slice(j * DH, (j + 1) * DH)
                    nc.vector.scalar_tensor_tensor(out=kd[h, 1, :, :, j], in0=kT_psum[h], scalar=qk_w[h, 2:3],
                                                   in1=kd[h, 0, :, :, j].bitcast(F32), op0=ALU.mult,
                                                   op1=ALU.subtract).then_inc(k_lo.sem, 1)

            def q(f, m):
                dve.wait_ge(q_hi.sem, q_hi.at(f, m + 1))
                lo(qT[:, 1, m], q_bank[m][:], qT[:, 0, m]).then_inc(q_lo.sem, 1)

            def q_mean(f):
                dve.wait_ge(ssq_done.sem, ssq_done.at(f))
                dve.wait_ge(q_r_done.sem, q_r_done.before(f))
                nc.vector.tensor_scalar(q_ve[:], ssq_ps, 1.0 / DH, EPS, ALU.mult, ALU.add
                                        ).then_inc(q_ve_done.sem, 1)

            def row_max(f, t):
                dve.wait_ge(s_ps.sem, s_ps.at(f, t + 1))
                dve.wait_ge(exp_done.sem, exp_done.before(f))
                nc.vector.tensor_reduce(s_max[:, t], s_bank[t][:, 0:HK].rearrange("p (h k) -> p h k", k=LK),
                                        AX.X, ALU.max).then_inc(s_max_done.sem, 1)
                dve.wait_ge(s_max_done.sem, s_max_done.at(f, t + 1))
                dve.wait_ge(q_r_done.sem, q_r_done.at(f))
                nc.vector.scalar_tensor_tensor(out=s_bias[:, t], in0=s_max[:, t], scalar=-1.0, in1=q_r[:, t],
                                               op0=ALU.mult, op1=ALU.mult).then_inc(s_bias_done.sem, 1)

            def inverse(f, t):
                dve.wait_ge(exp_done.sem, exp_done.at(f, t + 1))
                nc.vector.reciprocal(p_inv[:, t], p_sum[:, t]).then_inc(p_inv_done.sem, 1)

            def pT_part(f, t):
                dve.wait_ge(pT_hi.sem, pT_hi.at(f, t + 1))
                lo(pT[:, 1, t // SUB, :, t % SUB], s_bank[t][0:LK, :].rearrange("k (h q) -> k h q", h=H),
                   pT[:, 0, t // SUB, :, t % SUB]).then_inc(pT_lo.sem, 1)

            def o_part(f, m):
                dve.wait_ge(o_hi.sem, o_hi.at(f, m + 1))
                lo(oT[:, 1, m], o_bank[m][:], oT[:, 0, m]).then_inc(o_lo.sem, 1)

            def x2T_part(p, k):
                dve.wait_ge(x2T_hi.sem, x2T_hi.at(p, k + 1))
                lo(x2T[:, p.parity, 1, k], x2T_bank[k][:], x2T[:, p.parity, 0, k]).then_inc(x2T_lo.sem, 1)

            def route(p):
                n = [0]

                def after(k):
                    dve.wait_ge(top2.sem, top2.at(p, k))

                def did(ins):
                    n[0] += 1
                    ins.then_inc(top2.sem, 1)
                    return n[0]

                def bc(a):
                    return a.unsqueeze(2).to_broadcast([P, T, E])

                weight = first_weight[:].unsqueeze(1).to_broadcast([P, T, E])
                dve.wait_ge(lg_done.sem, lg_done.at(p))
                dve.wait_ge(gate_chain.sem, gate_chain.before(p))
                dve.wait_ge(pos_done.sem, pos_done.before(p))
                nc.vector.tensor_copy(lg_lo[:], lg_ps[:, :, 1]).then_inc(lg_lo_done.sem, 1)
                dve.wait_ge(lg_lo_done.sem, lg_lo_done.at(p))
                k = did(nc.vector.tensor_tensor(lg[:], lg_ps[:, :, 0], lg_lo[:], ALU.add))
                cur = lg
                for i in range(TOPK):
                    after(k)
                    k = did(nc.vector.tensor_reduce(top[:, i], cur[:], AX.X, ALU.max))
                    after(k)
                    if i == 1:
                        gap_at = did(nc.vector.tensor_tensor(gap[:], top[:, 1], top[:, 0], ALU.subtract))
                        assert gap_at == GAP_STEP
                    k = did(nc.vector.tensor_tensor(eq[:], cur[:], bc(top[:, i]), ALU.is_ge))
                    after(k)
                    k = did(nc.vector.tensor_tensor(rank[:], eq[:], weight, ALU.mult))
                    after(k)
                    k = did(nc.vector.tensor_reduce(first[:], rank[:], AX.X, ALU.max))
                    after(k)
                    k = did(nc.vector.tensor_tensor(mask[:, i], rank[:], bc(first[:]), ALU.is_equal))
                    after(k)
                    if i == 0:
                        k = did(nc.vector.scalar_tensor_tensor(out=lg2[:], in0=mask[:, 0], scalar=-BIG,
                                                               in1=lg[:], op0=ALU.mult, op1=ALU.add))
                        cur = lg2
                did(nc.vector.tensor_tensor(both[:], mask[:, 0], mask[:, 1], ALU.add))
                assert n[0] == ROUTE_STEPS, n[0]

            def gates(p):
                def did(ins):
                    ins.then_inc(gate_chain.sem, 1)

                def bc(a):
                    return a.unsqueeze(2).to_broadcast([P, T, E])

                dve.wait_ge(egap_done.sem, egap_done.at(p))
                did(nc.vector.tensor_scalar(den[:], egap[:], 1.0, None, ALU.add))
                dve.wait_ge(gate_chain.sem, gate_chain.at(p, 1))
                did(nc.vector.reciprocal(w_top[:, 0], den[:]))
                dve.wait_ge(gate_chain.sem, gate_chain.at(p, 2))
                did(nc.vector.tensor_tensor(w_top[:, 1], w_top[:, 0], egap[:], ALU.mult))
                did(nc.vector.tensor_tensor(g_part[:, 0], mask[:, 0], bc(w_top[:, 0]), ALU.mult))
                dve.wait_ge(gate_chain.sem, gate_chain.at(p, 3))
                did(nc.vector.tensor_tensor(g_part[:, 1], mask[:, 1], bc(w_top[:, 1]), ALU.mult))
                dve.wait_ge(gate_chain.sem, gate_chain.at(p, 5))
                did(nc.vector.tensor_tensor(g_all[:], g_part[:, 0], g_part[:, 1], ALU.add))
                dve.wait_ge(gate_chain.sem, gate_chain.at(p, 6))
                dve.wait_ge(pos_done.sem, pos_done.at(p))
                dve.wait_ge(v_added.sem, v_added.before(p, 2))
                dve.wait_ge(a_ready.sem, a_ready.before(p, 2))
                for b in range(BP):
                    did(nc.vector.scalar_tensor_tensor(
                        out=gate[:, p.parity, b * SUB:(b + 1) * SUB],
                        in0=pos_ps.rearrange("p (s b e) -> p b s e", s=SUB, b=BP)[:, b], scalar=float(CAP),
                        in1=g_all[:, b * SUB:(b + 1) * SUB], op0=ALU.is_lt, op1=ALU.mult))

            def experts(m, c):
                t, ep = c // (E // 2), c % (E // 2)
                dve.wait_ge(moe_ps.sem, moe_ps.at(m, c + 1))
                for i in range(2):
                    e = 2 * ep + i
                    if e == 0:
                        dve.wait_ge(gate_chain.sem, gate_chain.at(m))
                        dve.wait_ge(x1_done.sem, x1_done.at(m))
                        dve.wait_ge(y_done[t].sem, y_done[t].before(m))
                        src = x1[:, m.parity, t]
                    else:
                        dve.wait_ge(v_added.sem, v_added.at(m, c + i))
                        src = acc_v[:, t]
                    nc.vector.scalar_tensor_tensor(out=acc_v[:, t], in0=bkM[0][:, i * D:(i + 1) * D],
                                                   scalar=gate[:, m.parity, t, e:e + 1], in1=src,
                                                   op0=ALU.mult, op1=ALU.add).then_inc(v_added.sem, 1)

            def slot(k, m, p, f):
                if k == 0 and p:
                    o_part(p, 1)
                if k == 0 and f:
                    ln1(f)
                if k == 1 and f:
                    ctx_lo(f)
                if k == 1 and p:
                    residual(p, 0)
                if k == 1 and f:
                    ln1_shift(f)
                if k == 2 and p:
                    residual(p, 1)
                if k == 3 and f:
                    kv(f, 0)
                if k == 4 and p:
                    ln2_shift(p)
                if k == 4 and f:
                    xT_part(f, 0)
                    xT_part(f, 1)
                    kv(f, 1)
                if k == 6 and f:
                    k_scale(f)
                    q(f, 0)
                if k == 7 and f:
                    q(f, 1)
                if k == 7 and p:
                    x2T_part(p, 0)
                    x2T_part(p, 1)
                if k == 8 and f:
                    q_mean(f)
                    k_part(f)
                if k == 9 and f:
                    row_max(f, 0)
                    row_max(f, 1)
                    row_max(f, 2)
                    row_max(f, 3)
                if k == 11 and f:
                    inverse(f, 0)
                    inverse(f, 1)
                if k == 11 and p:
                    route(p)
                if k == 12 and f:
                    inverse(f, 2)
                    inverse(f, 3)
                if k == 13 and f:
                    pT_part(f, 0)
                    pT_part(f, 1)
                if k == 14 and f:
                    pT_part(f, 2)
                    pT_part(f, 3)
                if k == 14 and p:
                    gates(p)
                if k == 15 and f:
                    o_part(f, 0)
                if m and k % 2 == 0:
                    experts(m, k)

            def fill():
                for f, p in ((Pair(0, 0), None), (Pair(0, 1), Pair(0, 0))):
                    for k in range(SLOTS):
                        slot(k, None, p, f)

            def step(m, p, f, ahead):
                for k in range(SLOTS):
                    slot(k, m, p, f)

            pipeline(dve, fill, step)

        @block.tensor
        def _(pe):
            pe.wait_ge(const_ready, 4 + E + 3)
            pe.wait_ge(setup_v, 7)
            pe.wait_ge(stage_used, FRONT_WEIGHTS)

            def moe(m, c):
                t, ep = c // (E // 2), c % (E // 2)
                if c == 0:
                    pe.wait_ge(stage_used, len(weights))
                    pe.wait_ge(x2T_lo.sem, x2T_lo.at(m))
                if c % 2 == 0:
                    pe.wait_ge(v_added.sem, v_added.at(m, c))
                else:
                    pe.wait_ge(a_ready.sem, a_ready.at(m, c // 2))
                lhs = x2T[:, m.parity]
                product(bkM[c % 2][:], [
                    ([lhs[:, a, k, t * P:(t + 1) * P] for a in range(2)],
                     [we[:, a, k, ep * 512:(ep + 1) * 512] for a in range(2)]) for k in range(KC)]).then_inc(moe_ps.sem, 1)

            def fc(p, i):
                pe.wait_ge(o_lo.sem, o_lo.at(p))
                for t in range(2 * i, 2 * i + 2):
                    mm = product(fc_bank[i][:, (t % 2) * D:(t % 2 + 1) * D], [
                        ([oT[:, a, m, t * P:(t + 1) * P] for a in range(2)],
                         [wfc[:, a, m] for a in range(2)]) for m in range(KC)])
                mm.then_inc(fc_ps.sem, 1)

            def ctx_transpose(f):
                pe.wait_ge(ctx_sem[f.parity], 16 * f.half + 16)
                pe.wait_ge(pT_lo.sem, pT_lo.before(f))
                for k in range(KC):
                    for b in range(BP):
                        c0 = (k * BP + b) * LK
                        tr = pe.transpose(cT_psum[:, c0:c0 + LK], ctx_sb[:, f.parity, b, k * P:(k + 1) * P],
                                          ident[0:LK, 0:LK])
                tr.then_inc(cT_ps.sem, 1)

            def x_transpose(f):
                pe.wait_ge(xn1_done.sem, xn1_done.at(f))
                pe.wait_ge(x1_done.sem, x1_done.before(f))
                for k in range(KC):
                    for t in range(T):
                        tr = pe.transpose(xT_bank[k][:, t * P:(t + 1) * P], xn1[:, t, k * P:(k + 1) * P],
                                          ident[:])
                    tr.then_inc(xT_ps.sem, 1)

            def kv(f, b):
                pe.wait_ge(cT_lo.sem, cT_lo.at(f))
                product(kv_bank[b][0:LK, :], [
                    ([cT[:, a, k, b * LK:(b + 1) * LK] for a in range(2)],
                     [wkv[:, a, k] for a in range(2)]) for k in range(KC)]).then_inc(kv_ps.sem, 1)

            def q(f, m):
                pe.wait_ge(xT_lo.sem, xT_lo.at(f))
                product(q_bank[m][:], [
                    ([wq[:, a, k, m * P:(m + 1) * P] for a in range(2)],
                     [xT[:, a, k] for a in range(2)]) for k in range(KC)]).then_inc(q_ps.sem, 1)

            def k_transpose(f):
                pe.wait_ge(kn_done.sem, kn_done.at(f))
                for b in range(BP):
                    for m in range(KC):
                        tr = pe.transpose(kT_psum[:, b, m], kn[:, b, m * P:(m + 1) * P], ident[0:LK, 0:LK])
                tr.then_inc(kT_ps.sem, 1)

            def q_squares(f):
                pe.wait_ge(q_sq_done.sem, q_sq_done.at(f))
                pe.wait_ge(kn_done.sem, kn_done.at(f))
                for t in range(T):
                    for m in range(KC):
                        c0 = t * H + m * 2
                        mm = pe.matmul(ssq_ps[:, c0:c0 + 2], q_sq[:, m, t * P:(t + 1) * P], head_ones[:],
                                       start=True, stop=True)
                mm.then_inc(ssq_done.sem, 1)

            def scores(f, t):
                pe.wait_ge(k_lo.sem, k_lo.at(f))
                pe.wait_ge(q_lo.sem, q_lo.at(f))
                if t == T - 1:
                    pe.wait_ge(q_ve_done.sem, q_ve_done.at(f))
                for m in range(KC):
                    mm = product(s_bank[t][:, m * 2 * LK:(m + 1) * 2 * LK], [
                        ([qT[:, a, m, t * P:(t + 1) * P] for a in range(2)],
                         [kd[:, a, t // SUB, m].rearrange("p j k -> p (j k)") for a in range(2)])])
                mm.then_inc(s_ps.sem, 1)

            def p_transpose(f, t):
                pe.wait_ge(probs_done.sem, probs_done.at(f, t + 1))
                for h in range(H):
                    tr = pe.transpose(s_bank[t][0:LK, h * P:(h + 1) * P], probs[:, t, h * LK:(h + 1) * LK],
                                      ident[:])
                tr.then_inc(pT_ps.sem, 1)

            def attend(f, m, p):
                pe.wait_ge(v_lo.sem, v_lo.at(f))
                if m == 0 and p:
                    pe.wait_ge(x2T_lo.sem, x2T_lo.at(p))
                if m == 1 and p:
                    pe.wait_ge(gate_chain.sem, gate_chain.at(p))
                for b in range(BP):
                    if m == 0:
                        pe.wait_ge(pT_lo.sem, pT_lo.at(f, SUB * (b + 1)))
                    mm = product(o_bank[m][:, b * LQ:(b + 1) * LQ], [
                        ([vz[:, a, b, m, j * P:(j + 1) * P] for a in range(2)],
                         [pT[:, a, b, 2 * m + j].rearrange("k s q -> k (s q)") for a in range(2)])
                        for j in range(2)])
                mm.then_inc(o_ps.sem, 1)

            def x2_transpose(p, k):
                pe.wait_ge(xn2_done.sem, xn2_done.at(p))
                pe.wait_ge(o_lo.sem, o_lo.at(p))
                for t in range(T):
                    tr = pe.transpose(x2T_bank[k][:, t * P:(t + 1) * P], xn2[:, t, k * P:(k + 1) * P],
                                      ident[:])
                tr.then_inc(x2T_ps.sem, 1)

            def logits(p):
                pe.wait_ge(x2T_lo.sem, x2T_lo.at(p))
                for t in range(T):
                    for k in range(KC):
                        for a in range(2):
                            mm = pe.matmul(lg_ps[:, t].rearrange("p a e -> p (a e)"),
                                           x2T[:, p.parity, a, k, t * P:(t + 1) * P],
                                           wr[:, k].rearrange("p a e -> p (a e)"),
                                           start=(k == 0 and a == 0), stop=(k == KC - 1 and a == 1))
                mm.then_inc(lg_done.sem, 1)

            def positions(p):
                pe.wait_ge(top2.sem, top2.at(p))
                mk = both[:].rearrange("p (b s) e -> p s b e", s=SUB)
                pe.matmul(pos_ps[:, 0:BP * E], before[:], mk[:, 0], start=True, stop=False)
                pe.matmul(pos_ps[:, 0:BP * E], before[:], mk[:, 1], start=False, stop=True)
                pe.matmul(pos_ps[:, BP * E:], upto[:], mk[:, 0], start=True, stop=False)
                pe.matmul(pos_ps[:, BP * E:], before[:], mk[:, 1], start=False, stop=True).then_inc(pos_done.sem, 1)

            def slot(k, m, p, f):
                if m:
                    moe(m, k)
                if k == 0 and p:
                    fc(p, 0)
                if k == 0 and f:
                    ctx_transpose(f)
                if k == 1 and p:
                    fc(p, 1)
                if k == 2 and f:
                    kv(f, 0)
                if k == 3 and f:
                    kv(f, 1)
                    x_transpose(f)
                if k == 5 and f:
                    q(f, 0)
                if k == 6 and f:
                    q(f, 1)
                if k == 6 and p:
                    x2_transpose(p, 0)
                    x2_transpose(p, 1)
                if k == 7 and f:
                    q_squares(f)
                    k_transpose(f)
                if k == 8 and p:
                    logits(p)
                if k == 8 and f:
                    scores(f, 0)
                    scores(f, 1)
                if k == 9 and f:
                    scores(f, 2)
                    scores(f, 3)
                if k == 12 and f:
                    p_transpose(f, 0)
                    p_transpose(f, 1)
                if k == 13 and f:
                    p_transpose(f, 2)
                    p_transpose(f, 3)
                if k == 13 and p:
                    positions(p)
                if k == 14 and f:
                    attend(f, 0, p)
                if k == 15 and f:
                    attend(f, 1, p)

            def fill():
                for f, p in ((Pair(0, 0), None), (Pair(0, 1), Pair(0, 0))):
                    for k in range(SLOTS):
                        slot(k, None, p, f)

            def step(m, p, f, ahead):
                for k in range(SLOTS):
                    slot(k, m, p, f)

            pipeline(pe, fill, step)


INPUTS = ["x", "ctx_1024", "g_xattn", "g_ffn", "L0_xattn_Wq", "L0_xattn_Wkv", "L0_xattn_Wfc",
          "L0_xattn_fc_b", "L0_xattn_qn_w", "L0_xattn_kn_w", "L0_ffn_Wr", "L0_ffn_We"]


def kernel(**inputs):
    import numpy as np
    import concourse.bacc as bacc
    from concourse.bass_utils import run_bass_kernel_spmd

    nc = bacc.Bacc("TRN2", target_bir_lowering=False, num_devices=1)
    arrays, args = {}, []
    for name in INPUTS:
        a = np.ascontiguousarray(inputs[name])
        arrays[f"in_{name}"] = a
        args.append(nc.dram_tensor(f"in_{name}", a.shape, mybir.dt.from_np(a.dtype), kind="ExternalInput").ap())
    out = nc.dram_tensor("out", (B, LQ, D), F32, kind="ExternalOutput").ap()
    build(nc, *args, out)
    result = run_bass_kernel_spmd(nc, [arrays], core_ids=[0])
    return result.results[0]["out"]
```

```python
from contextlib import ExitStack

import concourse.bass as bass
from concourse import mybir

F32 = mybir.dt.float32
F32R = mybir.dt.float32r
BF16 = mybir.dt.bfloat16
ALU = mybir.AluOpType
ACT = mybir.ActivationFunctionType
AX = mybir.AxisListType

P = 128
B, LQ, D = 64, 256, 256
LK = 77
H, DH = 4, 64
E, TOPK = 8, 2
CAP = int(LQ * TOPK / E * 1.5) + 1
EPS = 1e-5
KC = D // P
BP = 2
PAIRS = B // BP
SUB = LQ // P
T = BP * SUB
TOK = T * P
HK = H * LK
SPLIT_TERMS = ((0, 0), (0, 1), (1, 0))
BIG = 3.0e38


class Pair:

    def __init__(self, j, c):
        self.n = 2 * j + c
        self.half = j + c // 2
        self.parity = c % 2


class Signal:

    def __init__(self, sem, per_pair, unit=1):
        self.sem, self.per_pair, self.unit = sem, per_pair, unit

    def at(self, pair, k=None):
        return (pair.n * self.per_pair + (self.per_pair if k is None else k)) * self.unit

    def before(self, pair, back=1):
        n = pair.n - (back - 1)
        if isinstance(n, int):
            n = max(n, 0)
        return n * (self.per_pair * self.unit)


def build(nc, x, ctx_in, g_xattn, g_ffn, Wq, Wkv, Wfc, fc_b, qn_w, kn_w, Wr, We, out):
    es = ExitStack()
    with es:
        def sb(name, shape, dt=F32):
            return es.enter_context(nc.sbuf_tensor(name, shape, dt))

        def bank(name):
            return es.enter_context(nc.psum_tensor(name, [P, 512], F32))

        def sem(name):
            return es.enter_context(nc.semaphore(name))

        def sig(name, per_pair, unit=1):
            return Signal(sem(name), per_pair, unit)

        x_v = x.rearrange("(n b) (q s) d -> n q b (s d)", b=BP, s=SUB)
        out_v = out.rearrange("(n b) (q s) d -> n q b (s d)", b=BP, s=SUB)
        ctx_v = ctx_in.rearrange("(n b) k d -> n k b d", b=BP)

        ident = sb("ident", [P, P])
        head_ones = sb("head_ones", [P, 2])
        before = sb("before", [P, P], BF16)
        upto = sb("upto", [P, P], BF16)
        first_weight = sb("first_weight", [P, E])
        minus_half = sb("minus_half", [P, 2 * 8])
        tanh_g = sb("tanh_g", [P, 2])
        bias_bc = sb("bias_bc", [P, D])
        bias_g = sb("bias_g", [P, D])
        qk_w = sb("qk_w", [P, 3])
        stage = sb("stage", [P, 2, E * D])
        stage_r = sb("stage_r", [P, KC, E])
        wq = sb("wq", [P, 2, KC, D], F32R)
        wkv = sb("wkv", [P, 2, KC, 2 * D], F32R)
        wfc = sb("wfc", [P, 2, KC, D], F32R)
        wr = sb("wr", [P, KC, 2, E], F32R)
        we = sb("we", [P, 2, KC, E * D], F32R)

        x_sb = sb("x_sb", [P, 2, T, D])
        ctx_sb = sb("ctx_sb", [LK, 2, BP, D])
        stats1 = sb("stats1", [P, T, 6])
        mv1 = sb("mv1", [P, T, 2])
        ve1 = sb("ve1", [P, T])
        rstd1 = sb("rstd1", [P, T])
        shift1 = sb("shift1", [P, T])
        xn1 = sb("xn1", [P, T, D])
        xb = sb("xb", [P, T, D])
        xT = sb("xT", [P, 2, KC, TOK], F32R)
        cT = sb("cT", [P, 2, KC, BP * LK], F32R)
        k_sq = sb("k_sq", [LK, BP, D])
        k_ss = sb("k_ss", [LK, BP * H])
        k_ve = sb("k_ve", [LK, BP * H])
        k_r = sb("k_r", [LK, BP * H])
        kn = sb("kn", [LK, BP, D])
        kd = sb("kd", [P, 2, BP, KC, 2, LK], F32R)
        vz = sb("vz", [LK, 2, BP, KC, 2 * P], F32R)
        qT = sb("qT", [P, 2, KC, TOK], F32R)
        q_sq = sb("q_sq", [P, KC, TOK])
        q_ve = sb("q_ve", [P, T * H])
        q_r = sb("q_r", [P, T, H])
        s_max = sb("s_max", [P, T, H])
        s_bias = sb("s_bias", [P, T, H])
        probs = sb("probs", [P, T, HK])
        p_sum = sb("p_sum", [P, T, H])
        p_inv = sb("p_inv", [P, T, H])
        pT = sb("pT", [LK, 2, BP, H, SUB, P], F32R)
        oT = sb("oT", [P, 2, KC, TOK], F32R)
        x1 = sb("x1", [P, 2, T, D])
        stats2 = sb("stats2", [P, T, 6])
        mv2 = sb("mv2", [P, T, 2])
        ve2 = sb("ve2", [P, T])
        rstd2 = sb("rstd2", [P, T])
        shift2 = sb("shift2", [P, T])
        xn2 = sb("xn2", [P, T, D])
        x2T = sb("x2T", [P, 2, 2, KC, TOK], F32R)
        lgT = sb("lgT", [2 * E, TOK])
        lg = sb("lg", [P, T, E])
        lg_lo = sb("lg_lo", [P, T, E])
        lg2 = sb("lg2", [P, T, E])
        eq = sb("eq", [P, T, E])
        rank = sb("rank", [P, T, E])
        first = sb("first", [P, T])
        top = sb("top", [P, 2, T])
        mask = sb("mask", [P, 2, T, E])
        both = sb("both", [P, T, E], BF16)
        gap = sb("gap", [P, T])
        egap = sb("egap", [P, T])
        den = sb("den", [P, T])
        w_top = sb("w_top", [P, 2, T])
        g_part = sb("g_part", [P, 2, T, E])
        g_all = sb("g_all", [P, T, E])
        gate = sb("gate", [P, 2, T, E])
        acc_v = sb("acc_v", [P, T, D])
        a_out = sb("a_out", [P, 2, E // 2, D])
        a_sum = sb("a_sum", [P, 2, D])
        y = sb("y", [P, T, D])

        bkA, bkB, bkC, bkD, bkE, bkF = (bank(f"bk{c}") for c in "ABCDEF")
        bkM = [bank("bkM0"), bank("bkM1")]
        cT_psum = bkE[:, 0:KC * BP * LK]
        kT_psum = bkD[:, 0:BP * KC * LK].rearrange("p (b m k) -> p b m k", b=BP, m=KC)
        ssq_ps = bkE[:, 0:T * H]
        lgT_ps = bkC[0:2 * E, :]
        lg_ps = bkC[:, 0:T * 2 * E].rearrange("p (t a e) -> p t a e", a=2, e=E)
        pos_ps = bkC[:, T * 2 * E:T * 3 * E]
        xT_bank = [bkA, bkB]
        q_bank = [bkA, bkB]
        kv_bank = [bkD, bkE]
        s_bank = [bkA, bkB, bkD, bkE]
        o_bank = [bkF, bkC]
        fc_bank = [bkA, bkB]
        x2T_bank = [bkF, bkC]

        ROUTE_HALF, GAP_STEP, ROUTE_STEPS = 7, 9, 14
        w_in = sem("w_in")
        stage_in = [sem(f"stage_in{n}") for n in range(6)]
        stage_used = sem("stage_used")
        const_ready = sem("const_ready")
        tanh_ready = sem("tanh_ready")
        hi_ready = sem("hi_ready")
        setup_v = sem("setup_v")
        waits_alone = sem("waits_alone")
        x_in = [sem("x_in0"), sem("x_in1")]
        ctx_sem = [sem("ctx_in0"), sem("ctx_in1")]
        y_out = [sig("y_out0", 1, 16), sig("y_out1", 1, 16)]
        stats1_done = sig("stats1_done", 4)
        var1_done = sig("var1_done", 5)
        rstd1_done = sig("rstd1_done", 1)
        shift1_done = sig("shift1_done", 1)
        xn1_done = sig("xn1_done", T)
        xb_done = sig("xb_done", T)
        xT_ps = sig("xT_ps", KC)
        xT_hi = sig("xT_hi", KC)
        xT_lo = sig("xT_lo", KC)
        cT_ps = sig("cT_ps", 1)
        cT_hi = sig("cT_hi", 1)
        cT_lo = sig("cT_lo", 1)
        kv_ps = sig("kv_ps", BP)
        k_sq_done = sig("k_sq_done", BP)
        v_hi = sig("v_hi", BP)
        v_lo = sig("v_lo", BP)
        k_ss_done = sig("k_ss_done", BP + 1)
        k_r_done = sig("k_r_done", 1)
        kn_done = sig("kn_done", BP)
        kT_ps = sig("kT_ps", 1)
        k_hi = sig("k_hi", 2)
        k_lo = sig("k_lo", 2)
        q_ps = sig("q_ps", KC)
        q_hi = sig("q_hi", KC)
        q_sq_done = sig("q_sq_done", KC)
        q_lo = sig("q_lo", KC)
        ssq_done = sig("ssq_done", 1)
        q_ve_done = sig("q_ve_done", 1)
        q_r_done = sig("q_r_done", 1)
        s_ps = sig("s_ps", T)
        s_max_done = sig("s_max_done", T)
        s_bias_done = sig("s_bias_done", T)
        exp_done = sig("exp_done", T)
        p_inv_done = sig("p_inv_done", T)
        probs_done = sig("probs_done", T)
        pT_ps = sig("pT_ps", T)
        pT_hi = sig("pT_hi", T)
        pT_lo = sig("pT_lo", T)
        o_ps = sig("o_ps", KC)
        o_hi = sig("o_hi", KC)
        o_lo = sig("o_lo", KC)
        fc_ps = sig("fc_ps", 2)
        x1_done = sig("x1_done", 2)
        stats2_done = sig("stats2_done", T)
        var2_done = sig("var2_done", T + 1)
        rstd2_done = sig("rstd2_done", 1)
        shift2_done = sig("shift2_done", 1)
        xn2_done = sig("xn2_done", T)
        x2T_ps = sig("x2T_ps", KC)
        x2T_hi = sig("x2T_hi", KC)
        x2T_lo = sig("x2T_lo", KC)
        lgT_ready = sig("lgT_ready", 1)
        lgT_copied = sig("lgT_copied", 1)
        lg_done = sig("lg_done", 1)
        lg_lo_done = sig("lg_lo_done", 1)
        top2 = sig("top2", ROUTE_STEPS)
        egap_done = sig("egap_done", 1)
        GATE_STEPS = 8
        gate_chain = sig("gate_chain", GATE_STEPS)
        pos_done = sig("pos_done", 1)
        CH = T * E // 2
        moe_ps = sig("moe_ps", CH)
        v_added = sig("v_added", CH)
        a_ready = sig("a_ready", CH // 2)
        a_summed = sig("a_summed", 3 * T)
        y_done = [sig(f"y_done{t}", 1) for t in range(T)]

        def chunked(a, n):
            return a.rearrange("p (k f) -> p k f", f=n)

        weights = [
            (chunked(stage[:, 0, KC * D:3 * KC * D], 2 * D), Wkv.rearrange("(k p) f -> p k f", p=P), None, wkv),
            (chunked(stage[:, 0, 0:KC * D], D), Wq.rearrange("(k p) f -> p k f", p=P), None, wq),
            (chunked(stage[:, 0, 3 * KC * D:4 * KC * D], D), Wfc.rearrange("(k p) f -> p k f", p=P),
             tanh_g[:, 0:1], wfc),
            (stage_r[:], Wr.rearrange("e (k p) -> p k e", p=P), None,
             wr[:].rearrange("p k a e -> p a k e")),
        ] + [(chunked(stage[:, 1 - k], D), We[:, k * P:(k + 1) * P, :].rearrange("e p f -> p e f"),
              tanh_g[:, 1:2], we[:, :, k].rearrange("p a (e f) -> p a e f", f=D)) for k in range(KC)]
        FRONT_WEIGHTS = 4
        UNGATED = 2
        STAGE0_USERS = 3

        SLOTS = T * E // 2

        def v_heads(b):
            return kv_bank[b][0:LK, D:2 * D].rearrange("k (m j d) -> k m j d", m=KC, j=2)

        def vz_heads(part, b):
            return vz[:, part, b].rearrange("k m (c d) -> k m c d", d=DH)[:, :, 0:4:3, :]

        def product(out, pairs):
            terms = [(l[a], r[b]) for l, r in pairs for a, b in SPLIT_TERMS]
            for i, (l, r) in enumerate(terms):
                mm = nc.tensor.matmul(out, l, r, start=(i == 0), stop=(i == len(terms) - 1))
            return mm

        ZEROS, BIAS_G, SETUP_V = 5, 6, 7

        LOOPS = (PAIRS - 4) // 2

        def tile_before_last(m, t):
            other = y_done[(t + 2) % T]
            return other.before(m) if t < 2 else other.at(m)

        def pipeline(engine, fill, step):
            fill()
            step(Pair(0, 0), Pair(0, 1), Pair(0, 2), Pair(0, 3))
            with engine.Fori(0, LOOPS) as j:
                step(Pair(j, 1), Pair(j, 2), Pair(j, 3), Pair(j, 4))
                step(Pair(j, 2), Pair(j, 3), Pair(j, 4), Pair(j, 5))
            step(Pair(LOOPS, 1), Pair(LOOPS, 2), Pair(LOOPS, 3), None)
            step(Pair(LOOPS, 2), Pair(LOOPS, 3), None, None)
            step(Pair(LOOPS, 3), None, None, None)

        block = es.enter_context(nc.Block())

        @block.sync
        def _(sp):
            def load(pair):
                for used in (xb_done, xn1_done, cT_ps):
                    sp.wait_ge(used.sem, used.before(pair, 2))
                    sp.sem_inc(waits_alone, 1)
                sp.dma_start(ctx_sb[:, pair.parity], ctx_v[pair.n]).then_inc(ctx_sem[pair.parity], 16)
                sp.dma_start(x_sb[:, pair.parity].rearrange("p (b s) d -> p b (s d)", b=BP),
                             x_v[pair.n]).then_inc(x_in[pair.parity], 16)

            def load_weights(ns):
                for n in ns:
                    view, src = weights[n][0:2]
                    if n == len(weights) - 1:
                        sp.wait_ge(stage_used, STAGE0_USERS)
                    if src.shape[-1] == E:
                        with nc.allow_non_contiguous_dma("router weights, once"):
                            for k in range(KC):
                                sp.dma_start(view[:, k], src[:, k]).then_inc(stage_in[n], 16)
                    else:
                        sp.dma_start(view, src).then_inc(stage_in[n], 16)

            load(Pair(0, 0))
            load_weights(range(UNGATED))
            with nc.allow_non_contiguous_dma("small one-time loads"):
                for dst, src in ((tanh_g[:, 0:1], g_xattn.partition_broadcast(P)),
                                 (tanh_g[:, 1:2], g_ffn.partition_broadcast(P)),
                                 (bias_bc[:], fc_b.partition_broadcast(P)),
                                 (qk_w[0:DH, 0:1], qn_w.rearrange("(d o) -> d o", o=1)),
                                 (qk_w[DH:P, 0:1], qn_w.rearrange("(d o) -> d o", o=1)),
                                 (qk_w[0:DH, 1:2], kn_w.rearrange("(d o) -> d o", o=1)),
                                 (qk_w[DH:P, 1:2], kn_w.rearrange("(d o) -> d o", o=1))):
                    sp.dma_start(dst, src).then_inc(w_in, 16)
            load_weights(range(UNGATED, FRONT_WEIGHTS))
            load(Pair(0, 1))
            load_weights(range(FRONT_WEIGHTS, len(weights)))

            def store(pair, b):
                for t in range(b * SUB, (b + 1) * SUB):
                    sp.wait_ge(y_done[t].sem, y_done[t].at(pair))
                    sp.sem_inc(waits_alone, 1)
                sp.dma_start(out_v[pair.n][:, b], y[:, b * SUB:(b + 1) * SUB].rearrange("p s d -> p (s d)")
                             ).then_inc(y_out[b].sem, 16)

            def step(m, p, f, ahead):
                if ahead:
                    load(ahead)
                store(m, 0)
                store(m, 1)

            pipeline(sp, lambda: load(Pair(0, 2)), step)
            for b in range(BP):
                sp.wait_ge(y_out[b].sem, 16 * PAIRS)

        @block.gpsimd
        def _(pool):
            pool.memset(ident[:], 0.0).then_inc(const_ready, 1)
            pool.memset(before[:], 1.0).then_inc(const_ready, 1)
            pool.memset(upto[:], 1.0).then_inc(const_ready, 1)
            pool.memset(minus_half[:], -0.5).then_inc(const_ready, 1)
            for e in range(E):
                pool.memset(first_weight[:, e:e + 1], float(E - e)).then_inc(const_ready, 1)
            pool.wait_ge(const_ready, 4 + E)
            pool.affine_select(out=ident[:], in_=ident[:], compare_op=ALU.not_equal, fill=1.0, base=0,
                               pattern=[[-1, P]], channel_multiplier=1).then_inc(const_ready, 1)
            pool.affine_select(out=before[:], in_=before[:], compare_op=ALU.is_gt, fill=0.0, base=0,
                               pattern=[[1, P]], channel_multiplier=-1).then_inc(const_ready, 1)
            pool.affine_select(out=upto[:], in_=upto[:], compare_op=ALU.is_ge, fill=0.0, base=0,
                               pattern=[[1, P]], channel_multiplier=-1).then_inc(const_ready, 1)

            def pow_m_half(dst, src, n, parts):
                return nc.gpsimd.tensor_tensor(dst, src, minus_half[0:parts, 0:n], ALU.pow)

            def ln1(f):
                pool.wait_ge(var1_done.sem, var1_done.at(f))
                pool.wait_ge(xn1_done.sem, xn1_done.before(f))
                pow_m_half(rstd1[:], ve1[:], T, P).then_inc(rstd1_done.sem, 1)

            def make_xb(f, t):
                pool.wait_ge(setup_v, BIAS_G)
                pool.wait_ge(x1_done.sem, x1_done.before(f))
                nc.gpsimd.tensor_tensor(xb[:, t], x_sb[:, f.parity, t], bias_g[:], ALU.add
                                        ).then_inc(xb_done.sem, 1)

            def ln2(p):
                pool.wait_ge(var2_done.sem, var2_done.at(p))
                pool.wait_ge(xn2_done.sem, xn2_done.before(p))
                pow_m_half(rstd2[:], ve2[:], T, P).then_inc(rstd2_done.sem, 1)

            def k_rsqrt(f):
                pool.wait_ge(k_ss_done.sem, k_ss_done.at(f))
                pow_m_half(k_r[:], k_ve[:], BP * H, LK).then_inc(k_r_done.sem, 1)

            def q_rsqrt(f):
                pool.wait_ge(q_ve_done.sem, q_ve_done.at(f))
                pow_m_half(q_r[:].rearrange("p t h -> p (t h)"), q_ve[:], T * H, P
                           ).then_inc(q_r_done.sem, 1)

            def normalise(f, t):
                pool.wait_ge(p_inv_done.sem, p_inv_done.at(f, t + 1))
                pr = probs[:, t].rearrange("p (h k) -> p h k", k=LK)
                nc.gpsimd.tensor_tensor(pr, pr, p_inv[:, t].unsqueeze(2).to_broadcast([P, H, LK]), ALU.mult
                                        ).then_inc(probs_done.sem, 1)

            def finish_tile(m, t):
                o, a = a_out[:, t % 2], a_sum[:, t % 2]
                for i in range(1, 4):
                    if i == 1:
                        pool.wait_ge(a_ready.sem, a_ready.at(m, 2 * t + 1))
                        pool.wait_ge(y_done[(t + 2) % T].sem, tile_before_last(m, t))
                    else:
                        pool.wait_ge(a_ready.sem, a_ready.at(m, 2 * t + 2))
                        pool.wait_ge(a_summed.sem, a_summed.at(m, 3 * t + i - 1))
                    nc.gpsimd.tensor_tensor(a, o[:, 0] if i == 1 else a, o[:, i], ALU.add
                                            ).then_inc(a_summed.sem, 1)
                pool.wait_ge(v_added.sem, v_added.at(m, 4 * (t + 1)))
                pool.wait_ge(a_summed.sem, a_summed.at(m, 3 * t + 3))
                pool.wait_ge(y_out[t // SUB].sem, y_out[t // SUB].before(m))
                nc.gpsimd.tensor_tensor(y[:, t], a, acc_v[:, t], ALU.add).then_inc(y_done[t].sem, 1)

            def slots(m, p, f):
                if f:
                    ln1(f)
                if p:
                    ln2(p)
                if f:
                    k_rsqrt(f)
                if m:
                    finish_tile(m, 0)
                if f:
                    make_xb(f, 0)
                    q_rsqrt(f)
                    make_xb(f, 1)
                    make_xb(f, 3)
                if m:
                    finish_tile(m, 1)
                if f:
                    make_xb(f, 2)
                    normalise(f, 0)
                    normalise(f, 1)
                    normalise(f, 2)
                    normalise(f, 3)
                if m:
                    finish_tile(m, 2)
                    finish_tile(m, 3)

            def fill():
                slots(None, None, Pair(0, 0))
                slots(None, Pair(0, 0), Pair(0, 1))

            def step(m, p, f, ahead):
                slots(m, p, f)

            pipeline(pool, fill, step)

        @block.scalar
        def _(act):
            def gates():
                act.wait_ge(w_in, 16 * 7)
                nc.scalar.activation(tanh_g[:], tanh_g[:], ACT.Tanh).then_inc(tanh_ready, 1)
                act.wait_ge(tanh_ready, 1)

            def weights_hi(ns):
                for n in ns:
                    view, src, scale, w = weights[n]
                    act.wait_ge(stage_in[n], 16 * (KC if src.shape[-1] == E else 1))
                    if scale is None:
                        nc.scalar.activation(w[:, 0], view, ACT.Copy).then_inc(hi_ready, 1)
                    else:
                        nc.scalar.activation(w[:, 0], view, ACT.Copy, scale=scale).then_inc(hi_ready, 1)

            def copy(dst, src, **kw):
                return nc.scalar.activation(dst, src, ACT.Copy, **kw)

            def ln1(f):
                act.wait_ge(shift1_done.sem, shift1_done.at(f))
                act.wait_ge(xT_ps.sem, xT_ps.before(f))
                for t in range(T):
                    nc.scalar.activation(xn1[:, t], x_sb[:, f.parity, t], ACT.Identity,
                                         scale=rstd1[:, t:t + 1], bias=shift1[:, t:t + 1]
                                         ).then_inc(xn1_done.sem, 1)

            def ln2(p):
                act.wait_ge(shift2_done.sem, shift2_done.at(p))
                act.wait_ge(x2T_ps.sem, x2T_ps.before(p))
                for t in range(T):
                    nc.scalar.activation(xn2[:, t], x1[:, p.parity, t], ACT.Identity,
                                         scale=rstd2[:, t:t + 1], bias=shift2[:, t:t + 1]
                                         ).then_inc(xn2_done.sem, 1)

            def ctx_hi(f):
                act.wait_ge(cT_ps.sem, cT_ps.at(f))
                act.wait_ge(kv_ps.sem, kv_ps.before(f))
                copy(cT[:, 0], cT_psum.rearrange("p (k c) -> p k c", k=KC)).then_inc(cT_hi.sem, 1)

            def xT_part(f, k):
                act.wait_ge(xT_ps.sem, xT_ps.at(f, k + 1))
                act.wait_ge(q_ps.sem, q_ps.before(f))
                copy(xT[:, 0, k], xT_bank[k][:]).then_inc(xT_hi.sem, 1)

            def kv(f, b):
                act.wait_ge(kv_ps.sem, kv_ps.at(f, b + 1))
                act.wait_ge(k_ss_done.sem, k_ss_done.before(f))
                nc.scalar.activation(k_sq[:, b], kv_bank[b][0:LK, 0:D], ACT.Square
                                     ).then_inc(k_sq_done.sem, 1)
                act.wait_ge(o_ps.sem, o_ps.before(f))
                copy(vz_heads(0, b), v_heads(b)).then_inc(v_hi.sem, 1)

            def q(f, m):
                act.wait_ge(q_ps.sem, q_ps.at(f, m + 1))
                act.wait_ge(ssq_done.sem, ssq_done.before(f))
                nc.scalar.activation(q_sq[:, m], q_bank[m][:], ACT.Square).then_inc(q_sq_done.sem, 1)
                act.wait_ge(s_ps.sem, s_ps.before(f))
                copy(qT[:, 0, m], q_bank[m][:]).then_inc(q_hi.sem, 1)

            def k_part(f):
                act.wait_ge(kT_ps.sem, kT_ps.at(f))
                act.wait_ge(s_ps.sem, s_ps.before(f))
                for j in range(2):
                    h = slice(j * DH, (j + 1) * DH)
                    copy(kd[h, 0, :, :, j], kT_psum[h], scale=qk_w[h, 2:3]).then_inc(k_hi.sem, 1)

            def exps(f, t):
                act.wait_ge(s_bias_done.sem, s_bias_done.at(f, t + 1))
                if t == 0:
                    act.wait_ge(pT_ps.sem, pT_ps.before(f))
                for h in range(H):
                    ins = nc.scalar.activation(probs[:, t, h * LK:(h + 1) * LK],
                                               s_bank[t][:, h * LK:(h + 1) * LK], ACT.Exp,
                                               scale=q_r[:, t, h:h + 1], bias=s_bias[:, t, h:h + 1],
                                               accum_out=p_sum[:, t, h:h + 1])
                ins.then_inc(exp_done.sem, 1)

            def pT_part(f, t):
                act.wait_ge(pT_ps.sem, pT_ps.at(f, t + 1))
                act.wait_ge(o_ps.sem, o_ps.before(f))
                copy(pT[:, 0, t // SUB, :, t % SUB], s_bank[t][0:LK, :].rearrange("k (h q) -> k h q", h=H)
                     ).then_inc(pT_hi.sem, 1)

            def o_part(f, m):
                act.wait_ge(o_ps.sem, o_ps.at(f, m + 1))
                act.wait_ge(fc_ps.sem, fc_ps.before(f))
                copy(oT[:, 0, m], o_bank[m][:]).then_inc(o_hi.sem, 1)

            def x2T_part(p, k):
                act.wait_ge(x2T_ps.sem, x2T_ps.at(p, k + 1))
                act.wait_ge(moe_ps.sem, moe_ps.before(p, 2))
                act.wait_ge(lg_done.sem, lg_done.before(p, 2))
                copy(x2T[:, p.parity, 0, k], x2T_bank[k][:]).then_inc(x2T_hi.sem, 1)

            def logits(p):
                act.wait_ge(lgT_ready.sem, lgT_ready.at(p))
                act.wait_ge(lg_done.sem, lg_done.before(p))
                copy(lgT[:], lgT_ps).then_inc(lgT_copied.sem, 1)

            def router_exp(p):
                act.wait_ge(top2.sem, top2.at(p, GAP_STEP))
                act.wait_ge(gate_chain.sem, gate_chain.before(p))
                nc.scalar.activation(egap[:], gap[:], ACT.Exp).then_inc(egap_done.sem, 1)

            def experts(m, c):
                t = c // (E // 2)
                act.wait_ge(moe_ps.sem, moe_ps.at(m, c + 1))
                act.wait_ge(gate_chain.sem, gate_chain.at(m))
                act.wait_ge(y_done[(t + 2) % T].sem, tile_before_last(m, t))
                for i in range(2):
                    e = 2 * (c % (E // 2)) + i
                    ins = nc.scalar.activation(a_out[:, t % 2, (e // 4) * 2 + i],
                                               bkM[1][:, i * D:(i + 1) * D], ACT.Copy,
                                               scale=gate[:, m.parity, t, e:e + 1])
                ins.then_inc(a_ready.sem, 1)

            def slot(k, m, p, f):
                if k == 0 and p:
                    o_part(p, 1)
                if k == 1:
                    if f:
                        ctx_hi(f)
                    if m:
                        experts(m, k)
                if k == 3:
                    if f:
                        ln1(f)
                        kv(f, 0)
                    if m:
                        experts(m, k)
                if k == 4:
                    if f:
                        xT_part(f, 0)
                        xT_part(f, 1)
                        kv(f, 1)
                    if p:
                        ln2(p)
                if k == 5 and m:
                    experts(m, k)
                if k == 7:
                    if f:
                        q(f, 0)
                        q(f, 1)
                    if p:
                        x2T_part(p, 0)
                        x2T_part(p, 1)
                    if m:
                        experts(m, k)
                if k == 8 and f:
                    k_part(f)
                if k == 9:
                    if p:
                        logits(p)
                    if f:
                        exps(f, 0)
                    if m:
                        experts(m, k)
                    if f:
                        exps(f, 1)
                if k == 11:
                    if f:
                        exps(f, 2)
                    if m:
                        experts(m, k)
                if k == 12 and f:
                    exps(f, 3)
                if k == 13:
                    if f:
                        pT_part(f, 0)
                        pT_part(f, 1)
                    if p:
                        router_exp(p)
                    if m:
                        experts(m, k)
                    if f:
                        pT_part(f, 2)
                        pT_part(f, 3)
                if k == 15:
                    if m:
                        experts(m, k)
                    if f:
                        o_part(f, 0)

            def fill():
                for f, p in ((Pair(0, 0), None), (Pair(0, 1), Pair(0, 0))):
                    for k in range(SLOTS):
                        slot(k, None, p, f)
                        if k == 2 and p is None:
                            weights_hi(range(UNGATED))
                            gates()
                            weights_hi(range(UNGATED, FRONT_WEIGHTS))
                        if k in (7, 8) and p is None:
                            weights_hi([FRONT_WEIGHTS + k - 7])

            def step(m, p, f, ahead):
                for k in range(SLOTS):
                    slot(k, m, p, f)

            pipeline(act, fill, step)

        @block.vector
        def _(dve):
            dve.memset(head_ones[:], 0.0).then_inc(setup_v, 1)
            dve.memset(kd[:].bitcast(F32).rearrange("p a b c d e -> p (a b c d e)"), 0.0).then_inc(setup_v, 1)
            dve.memset(vz[:].bitcast(F32).rearrange("p a b c d -> p (a b c d)"), 0.0).then_inc(setup_v, 1)
            dve.wait_ge(setup_v, 1)
            for j in range(2):
                dve.memset(head_ones[j * DH:(j + 1) * DH, j:j + 1], 1.0).then_inc(setup_v, 1)

            def gated_constants():
                dve.wait_ge(tanh_ready, 1)
                nc.vector.tensor_scalar(bias_g[:], bias_bc[:], tanh_g[:, 0:1], None, ALU.mult
                                        ).then_inc(setup_v, 1)
                nc.vector.scalar_tensor_tensor(out=qk_w[:, 2:3], in0=qk_w[:, 0:1], scalar=float(DH) ** -0.5,
                                               in1=qk_w[:, 1:2], op0=ALU.mult, op1=ALU.mult
                                               ).then_inc(setup_v, 1)

            def weights_lo(ns):
                for n in ns:
                    view, _, scale, w = weights[n]
                    dve.wait_ge(hi_ready, n + 1)
                    if scale is None:
                        nc.vector.tensor_tensor(w[:, 1], view, w[:, 0].bitcast(F32), ALU.subtract
                                                ).then_inc(stage_used, 1)
                    else:
                        nc.vector.scalar_tensor_tensor(out=w[:, 1], in0=view, scalar=scale,
                                                       in1=w[:, 0].bitcast(F32), op0=ALU.mult,
                                                       op1=ALU.subtract).then_inc(stage_used, 1)

            def lo(dst, src, hi):
                return nc.vector.tensor_tensor(dst, src, hi.bitcast(F32), ALU.subtract)

            def layernorm_stats(pair, src, stats, mv, ve, stats_done, var_done, tiles):
                for t in tiles:
                    nc.vector.bn_stats(stats[:, t], src[:, t]).then_inc(stats_done.sem, 1)
                for t in tiles:
                    dve.wait_ge(stats_done.sem, stats_done.at(pair, t + 1))
                    dve.sem_inc(waits_alone, 1)
                    nc.vector.bn_aggr(mv[:, t], stats[:, t]).then_inc(var_done.sem, 1)
                if tiles[-1] == T - 1:
                    dve.wait_ge(var_done.sem, var_done.at(pair, T))
                    nc.vector.tensor_scalar(ve[:], mv[:, :, 1], EPS, None, ALU.add).then_inc(var_done.sem, 1)

            def ln1(f):
                dve.wait_ge(x_in[f.parity], 16 * f.half + 16)
                dve.wait_ge(xn1_done.sem, xn1_done.before(f))
                layernorm_stats(f, x_sb[:, f.parity], stats1, mv1, ve1, stats1_done, var1_done, range(T))

            def shift(mv, rstd, dst):
                return nc.vector.scalar_tensor_tensor(out=dst, in0=mv[:, :, 0], scalar=-1.0, in1=rstd[:],
                                                      op0=ALU.mult, op1=ALU.mult)

            def ln1_shift(f):
                dve.wait_ge(rstd1_done.sem, rstd1_done.at(f))
                shift(mv1, rstd1, shift1[:]).then_inc(shift1_done.sem, 1)

            def ln2_shift(p):
                dve.wait_ge(rstd2_done.sem, rstd2_done.at(p))
                shift(mv2, rstd2, shift2[:]).then_inc(shift2_done.sem, 1)

            def residual(p, i):
                dve.wait_ge(fc_ps.sem, fc_ps.at(p, i + 1))
                dve.wait_ge(xb_done.sem, xb_done.at(p))
                if i == 0:
                    dve.wait_ge(xn2_done.sem, xn2_done.before(p))
                dve.wait_ge(v_added.sem, v_added.before(p, 2))
                ts = slice(2 * i, 2 * i + 2)
                nc.vector.tensor_tensor(x1[:, p.parity, ts], fc_bank[i][:].rearrange("p (t d) -> p t d", d=D),
                                        xb[:, ts], ALU.add).then_inc(x1_done.sem, 1)
                dve.wait_ge(x1_done.sem, x1_done.at(p, i + 1))
                layernorm_stats(p, x1[:, p.parity], stats2, mv2, ve2, stats2_done, var2_done,
                                range(2 * i, 2 * i + 2))

            def ctx_lo(f):
                dve.wait_ge(cT_hi.sem, cT_hi.at(f))
                lo(cT[:, 1], cT_psum.rearrange("p (k c) -> p k c", k=KC), cT[:, 0]).then_inc(cT_lo.sem, 1)

            def xT_part(f, k):
                dve.wait_ge(xT_hi.sem, xT_hi.at(f, k + 1))
                lo(xT[:, 1, k], xT_bank[k][:], xT[:, 0, k]).then_inc(xT_lo.sem, 1)

            def kv(f, b):
                dve.wait_ge(k_sq_done.sem, k_sq_done.at(f, b + 1))
                nc.vector.tensor_reduce(k_ss[:, b * H:(b + 1) * H], k_sq[:, b].rearrange("k (h d) -> k h d", d=DH),
                                        AX.X, ALU.add).then_inc(k_ss_done.sem, 1)
                dve.wait_ge(v_hi.sem, v_hi.at(f, b + 1))
                lo(vz_heads(1, b), v_heads(b), vz_heads(0, b)).then_inc(v_lo.sem, 1)
                if b == BP - 1:
                    dve.wait_ge(k_ss_done.sem, k_ss_done.at(f, BP))
                    nc.vector.tensor_scalar(k_ve[:], k_ss[:], 1.0 / DH, EPS, ALU.mult, ALU.add
                                            ).then_inc(k_ss_done.sem, 1)

            def k_scale(f):
                dve.wait_ge(k_r_done.sem, k_r_done.at(f))
                for b in range(BP):
                    nc.vector.tensor_tensor(
                        kn[:, b].rearrange("k (h d) -> k h d", d=DH),
                        kv_bank[b][0:LK, 0:D].rearrange("k (h d) -> k h d", d=DH),
                        k_r[:, b * H:(b + 1) * H].unsqueeze(2).to_broadcast([LK, H, DH]), ALU.mult
                    ).then_inc(kn_done.sem, 1)

            def k_part(f):
                for j in range(2):
                    dve.wait_ge(k_hi.sem, k_hi.at(f, j + 1))
                    h = slice(j * DH, (j + 1) * DH)
                    nc.vector.scalar_tensor_tensor(out=kd[h, 1, :, :, j], in0=kT_psum[h], scalar=qk_w[h, 2:3],
                                                   in1=kd[h, 0, :, :, j].bitcast(F32), op0=ALU.mult,
                                                   op1=ALU.subtract).then_inc(k_lo.sem, 1)

            def q(f, m):
                dve.wait_ge(q_hi.sem, q_hi.at(f, m + 1))
                lo(qT[:, 1, m], q_bank[m][:], qT[:, 0, m]).then_inc(q_lo.sem, 1)

            def q_mean(f):
                dve.wait_ge(ssq_done.sem, ssq_done.at(f))
                dve.wait_ge(q_r_done.sem, q_r_done.before(f))
                nc.vector.tensor_scalar(q_ve[:], ssq_ps, 1.0 / DH, EPS, ALU.mult, ALU.add
                                        ).then_inc(q_ve_done.sem, 1)

            def row_max(f, t):
                dve.wait_ge(s_ps.sem, s_ps.at(f, t + 1))
                dve.wait_ge(exp_done.sem, exp_done.before(f))
                nc.vector.tensor_reduce(s_max[:, t], s_bank[t][:, 0:HK].rearrange("p (h k) -> p h k", k=LK),
                                        AX.X, ALU.max).then_inc(s_max_done.sem, 1)
                dve.wait_ge(s_max_done.sem, s_max_done.at(f, t + 1))
                dve.wait_ge(q_r_done.sem, q_r_done.at(f))
                nc.vector.scalar_tensor_tensor(out=s_bias[:, t], in0=s_max[:, t], scalar=-1.0, in1=q_r[:, t],
                                               op0=ALU.mult, op1=ALU.mult).then_inc(s_bias_done.sem, 1)

            def inverse(f, t):
                dve.wait_ge(exp_done.sem, exp_done.at(f, t + 1))
                nc.vector.reciprocal(p_inv[:, t], p_sum[:, t]).then_inc(p_inv_done.sem, 1)

            def pT_part(f, t):
                dve.wait_ge(pT_hi.sem, pT_hi.at(f, t + 1))
                lo(pT[:, 1, t // SUB, :, t % SUB], s_bank[t][0:LK, :].rearrange("k (h q) -> k h q", h=H),
                   pT[:, 0, t // SUB, :, t % SUB]).then_inc(pT_lo.sem, 1)

            def o_part(f, m):
                dve.wait_ge(o_hi.sem, o_hi.at(f, m + 1))
                lo(oT[:, 1, m], o_bank[m][:], oT[:, 0, m]).then_inc(o_lo.sem, 1)

            def x2T_part(p, k):
                dve.wait_ge(x2T_hi.sem, x2T_hi.at(p, k + 1))
                lo(x2T[:, p.parity, 1, k], x2T_bank[k][:], x2T[:, p.parity, 0, k]).then_inc(x2T_lo.sem, 1)

            def route(p, i):
                steps = [0 if i == 0 else ROUTE_HALF]

                def after():
                    dve.wait_ge(top2.sem, top2.at(p, steps[0]))

                def did(ins):
                    steps[0] += 1
                    ins.then_inc(top2.sem, 1)

                def bc(a):
                    return a.unsqueeze(2).to_broadcast([P, T, E])

                weight = first_weight[:].unsqueeze(1).to_broadcast([P, T, E])
                if i == 0:
                    dve.wait_ge(lg_done.sem, lg_done.at(p))
                    dve.wait_ge(gate_chain.sem, gate_chain.before(p))
                    dve.wait_ge(pos_done.sem, pos_done.before(p))
                    nc.vector.tensor_copy(lg_lo[:], lg_ps[:, :, 1]).then_inc(lg_lo_done.sem, 1)
                    dve.wait_ge(lg_lo_done.sem, lg_lo_done.at(p))
                    did(nc.vector.tensor_tensor(lg[:], lg_ps[:, :, 0], lg_lo[:], ALU.add))
                cur = (lg, lg2)[i]
                after()
                did(nc.vector.tensor_reduce(top[:, i], cur[:], AX.X, ALU.max))
                after()
                if i == 1:
                    did(nc.vector.tensor_tensor(gap[:], top[:, 1], top[:, 0], ALU.subtract))
                    assert steps[0] == GAP_STEP
                did(nc.vector.tensor_tensor(eq[:], cur[:], bc(top[:, i]), ALU.is_ge))
                after()
                did(nc.vector.tensor_tensor(rank[:], eq[:], weight, ALU.mult))
                after()
                did(nc.vector.tensor_reduce(first[:], rank[:], AX.X, ALU.max))
                after()
                did(nc.vector.tensor_tensor(mask[:, i], rank[:], bc(first[:]), ALU.is_equal))
                after()
                if i == 0:
                    did(nc.vector.scalar_tensor_tensor(out=lg2[:], in0=mask[:, 0], scalar=-BIG,
                                                       in1=lg[:], op0=ALU.mult, op1=ALU.add))
                else:
                    did(nc.vector.tensor_tensor(both[:], mask[:, 0], mask[:, 1], ALU.add))
                assert steps[0] == (ROUTE_HALF, ROUTE_STEPS)[i]

            def gates(p):
                def did(ins):
                    ins.then_inc(gate_chain.sem, 1)

                def bc(a):
                    return a.unsqueeze(2).to_broadcast([P, T, E])

                dve.wait_ge(egap_done.sem, egap_done.at(p))
                did(nc.vector.tensor_scalar(den[:], egap[:], 1.0, None, ALU.add))
                dve.wait_ge(gate_chain.sem, gate_chain.at(p, 1))
                did(nc.vector.reciprocal(w_top[:, 0], den[:]))
                dve.wait_ge(gate_chain.sem, gate_chain.at(p, 2))
                did(nc.vector.tensor_tensor(w_top[:, 1], w_top[:, 0], egap[:], ALU.mult))
                did(nc.vector.tensor_tensor(g_part[:, 0], mask[:, 0], bc(w_top[:, 0]), ALU.mult))
                dve.wait_ge(gate_chain.sem, gate_chain.at(p, 3))
                did(nc.vector.tensor_tensor(g_part[:, 1], mask[:, 1], bc(w_top[:, 1]), ALU.mult))
                dve.wait_ge(gate_chain.sem, gate_chain.at(p, 5))
                did(nc.vector.tensor_tensor(g_all[:], g_part[:, 0], g_part[:, 1], ALU.add))
                dve.wait_ge(gate_chain.sem, gate_chain.at(p, 6))
                dve.wait_ge(pos_done.sem, pos_done.at(p))
                dve.wait_ge(v_added.sem, v_added.before(p, 2))
                dve.wait_ge(a_ready.sem, a_ready.before(p, 2))
                for b in range(BP):
                    did(nc.vector.scalar_tensor_tensor(
                        out=gate[:, p.parity, b * SUB:(b + 1) * SUB],
                        in0=pos_ps.rearrange("p (s b e) -> p b s e", s=SUB, b=BP)[:, b], scalar=float(CAP),
                        in1=g_all[:, b * SUB:(b + 1) * SUB], op0=ALU.is_lt, op1=ALU.mult))

            def experts(m, c):
                t, ep = c // (E // 2), c % (E // 2)
                dve.wait_ge(moe_ps.sem, moe_ps.at(m, c + 1))
                for i in range(2):
                    e = 2 * ep + i
                    if e == 0:
                        dve.wait_ge(gate_chain.sem, gate_chain.at(m))
                        dve.wait_ge(x1_done.sem, x1_done.at(m))
                        dve.wait_ge(y_done[t].sem, y_done[t].before(m))
                        src = x1[:, m.parity, t]
                    else:
                        dve.wait_ge(v_added.sem, v_added.at(m, c + i))
                        src = acc_v[:, t]
                    nc.vector.scalar_tensor_tensor(out=acc_v[:, t], in0=bkM[0][:, i * D:(i + 1) * D],
                                                   scalar=gate[:, m.parity, t, e:e + 1], in1=src,
                                                   op0=ALU.mult, op1=ALU.add).then_inc(v_added.sem, 1)

            def slot(k, m, p, f):
                if k == 0:
                    if p:
                        o_part(p, 1)
                    if m:
                        experts(m, k)
                    if f:
                        ln1(f)
                if k == 1 and f:
                    ctx_lo(f)
                if k == 2:
                    if p:
                        residual(p, 0)
                    if f:
                        ln1_shift(f)
                    if p:
                        residual(p, 1)
                    if m:
                        experts(m, k)
                if k == 3:
                    if p:
                        ln2_shift(p)
                    if f:
                        kv(f, 0)
                if k == 4:
                    if f:
                        xT_part(f, 0)
                        xT_part(f, 1)
                        kv(f, 1)
                    if m:
                        experts(m, k)
                if k == 5 and f:
                    k_scale(f)
                if k == 6:
                    if f:
                        q(f, 0)
                    if m:
                        experts(m, k)
                if k == 7:
                    if f:
                        q(f, 1)
                    if p:
                        x2T_part(p, 0)
                        x2T_part(p, 1)
                if k == 8:
                    if f:
                        q_mean(f)
                        k_part(f)
                    if m:
                        experts(m, k)
                if k == 9 and f:
                    row_max(f, 0)
                    row_max(f, 1)
                    row_max(f, 2)
                    row_max(f, 3)
                if k == 10 and m:
                    experts(m, k)
                if k == 11:
                    if f:
                        inverse(f, 0)
                    if p:
                        route(p, 0)
                    if f:
                        inverse(f, 1)
                        inverse(f, 2)
                if k == 12:
                    if m:
                        experts(m, k)
                    if f:
                        inverse(f, 3)
                    if p:
                        route(p, 1)
                if k == 13 and f:
                    pT_part(f, 0)
                    pT_part(f, 1)
                if k == 14:
                    if f:
                        pT_part(f, 2)
                        pT_part(f, 3)
                    if p:
                        gates(p)
                    if m:
                        experts(m, k)
                    if f:
                        o_part(f, 0)

            def fill():
                for f, p in ((Pair(0, 0), None), (Pair(0, 1), Pair(0, 0))):
                    for k in range(SLOTS):
                        slot(k, None, p, f)
                        if k == 2 and p is None:
                            weights_lo(range(UNGATED))
                            gated_constants()
                            weights_lo(range(UNGATED, FRONT_WEIGHTS))
                        if k in (8, 12) and p is None:
                            weights_lo([FRONT_WEIGHTS + (k == 12)])

            def step(m, p, f, ahead):
                for k in range(SLOTS):
                    slot(k, m, p, f)

            pipeline(dve, fill, step)

        @block.tensor
        def _(pe):
            pe.wait_ge(const_ready, 4 + E + 3)

            def moe(m, c):
                t, ep = c // (E // 2), c % (E // 2)
                if c == 0:
                    pe.wait_ge(stage_used, len(weights))
                    pe.wait_ge(x2T_lo.sem, x2T_lo.at(m))
                if c % 2 == 0:
                    pe.wait_ge(v_added.sem, v_added.at(m, c))
                else:
                    pe.wait_ge(a_ready.sem, a_ready.at(m, c // 2))
                lhs = x2T[:, m.parity]
                product(bkM[c % 2][:], [
                    ([lhs[:, a, k, t * P:(t + 1) * P] for a in range(2)],
                     [we[:, a, k, ep * 512:(ep + 1) * 512] for a in range(2)]) for k in range(KC)]).then_inc(moe_ps.sem, 1)

            def fc(p, i):
                pe.wait_ge(o_lo.sem, o_lo.at(p))
                for t in range(2 * i, 2 * i + 2):
                    mm = product(fc_bank[i][:, (t % 2) * D:(t % 2 + 1) * D], [
                        ([oT[:, a, m, t * P:(t + 1) * P] for a in range(2)],
                         [wfc[:, a, m] for a in range(2)]) for m in range(KC)])
                mm.then_inc(fc_ps.sem, 1)

            def ctx_transpose(f):
                pe.wait_ge(ctx_sem[f.parity], 16 * f.half + 16)
                pe.wait_ge(pT_lo.sem, pT_lo.before(f))
                for k in range(KC):
                    for b in range(BP):
                        c0 = (k * BP + b) * LK
                        tr = pe.transpose(cT_psum[:, c0:c0 + LK], ctx_sb[:, f.parity, b, k * P:(k + 1) * P],
                                          ident[0:LK, 0:LK])
                tr.then_inc(cT_ps.sem, 1)

            def x_transpose(f):
                pe.wait_ge(xn1_done.sem, xn1_done.at(f))
                pe.wait_ge(x1_done.sem, x1_done.before(f))
                for k in range(KC):
                    for t in range(T):
                        tr = pe.transpose(xT_bank[k][:, t * P:(t + 1) * P], xn1[:, t, k * P:(k + 1) * P],
                                          ident[:])
                    tr.then_inc(xT_ps.sem, 1)

            def kv(f, b):
                pe.wait_ge(cT_lo.sem, cT_lo.at(f))
                product(kv_bank[b][0:LK, :], [
                    ([cT[:, a, k, b * LK:(b + 1) * LK] for a in range(2)],
                     [wkv[:, a, k] for a in range(2)]) for k in range(KC)]).then_inc(kv_ps.sem, 1)

            def q(f, m):
                pe.wait_ge(xT_lo.sem, xT_lo.at(f))
                product(q_bank[m][:], [
                    ([wq[:, a, k, m * P:(m + 1) * P] for a in range(2)],
                     [xT[:, a, k] for a in range(2)]) for k in range(KC)]).then_inc(q_ps.sem, 1)

            def k_transpose(f):
                pe.wait_ge(kn_done.sem, kn_done.at(f))
                for b in range(BP):
                    for m in range(KC):
                        tr = pe.transpose(kT_psum[:, b, m], kn[:, b, m * P:(m + 1) * P], ident[0:LK, 0:LK])
                tr.then_inc(kT_ps.sem, 1)

            def q_squares(f):
                pe.wait_ge(q_sq_done.sem, q_sq_done.at(f))
                pe.wait_ge(kn_done.sem, kn_done.at(f))
                for t in range(T):
                    for m in range(KC):
                        c0 = t * H + m * 2
                        mm = pe.matmul(ssq_ps[:, c0:c0 + 2], q_sq[:, m, t * P:(t + 1) * P], head_ones[:],
                                       start=True, stop=True)
                mm.then_inc(ssq_done.sem, 1)

            def scores(f, t):
                pe.wait_ge(k_lo.sem, k_lo.at(f))
                pe.wait_ge(q_lo.sem, q_lo.at(f))
                if t == T - 1:
                    pe.wait_ge(q_ve_done.sem, q_ve_done.at(f))
                for m in range(KC):
                    mm = product(s_bank[t][:, m * 2 * LK:(m + 1) * 2 * LK], [
                        ([qT[:, a, m, t * P:(t + 1) * P] for a in range(2)],
                         [kd[:, a, t // SUB, m].rearrange("p j k -> p (j k)") for a in range(2)])])
                mm.then_inc(s_ps.sem, 1)

            def p_transpose(f, t):
                pe.wait_ge(probs_done.sem, probs_done.at(f, t + 1))
                for h in range(H):
                    tr = pe.transpose(s_bank[t][0:LK, h * P:(h + 1) * P], probs[:, t, h * LK:(h + 1) * LK],
                                      ident[:])
                tr.then_inc(pT_ps.sem, 1)

            def attend(f, m, b, p):
                pe.wait_ge(v_lo.sem, v_lo.at(f))
                if m == 0:
                    if p and b == 0:
                        pe.wait_ge(x2T_lo.sem, x2T_lo.at(p))
                    pe.wait_ge(pT_lo.sem, pT_lo.at(f, SUB * (b + 1)))
                elif p and b == 0:
                    pe.wait_ge(gate_chain.sem, gate_chain.at(p))
                mm = product(o_bank[m][:, b * LQ:(b + 1) * LQ], [
                    ([vz[:, a, b, m, j * P:(j + 1) * P] for a in range(2)],
                     [pT[:, a, b, 2 * m + j].rearrange("k s q -> k (s q)") for a in range(2)])
                    for j in range(2)])
                if b == BP - 1:
                    mm.then_inc(o_ps.sem, 1)

            def x2_transpose(p, k):
                pe.wait_ge(xn2_done.sem, xn2_done.at(p))
                pe.wait_ge(o_lo.sem, o_lo.at(p))
                for t in range(T):
                    tr = pe.transpose(x2T_bank[k][:, t * P:(t + 1) * P], xn2[:, t, k * P:(k + 1) * P],
                                      ident[:])
                tr.then_inc(x2T_ps.sem, 1)

            def logits(p):
                pe.wait_ge(x2T_lo.sem, x2T_lo.at(p))
                for k in range(KC):
                    for a in range(2):
                        mm = pe.matmul(lgT_ps, wr[:, k].rearrange("p a e -> p (a e)"), x2T[:, p.parity, a, k],
                                       start=(k == 0 and a == 0), stop=(k == KC - 1 and a == 1))
                mm.then_inc(lgT_ready.sem, 1)

            def logits_transpose(p):
                pe.wait_ge(lgT_copied.sem, lgT_copied.at(p))
                pe.sem_inc(waits_alone, 1)
                for t in range(T):
                    tr = pe.transpose(lg_ps[:, t].rearrange("p a e -> p (a e)"), lgT[:, t * P:(t + 1) * P],
                                      ident[0:2 * E, 0:2 * E])
                tr.then_inc(lg_done.sem, 1)

            def positions(p):
                pe.wait_ge(top2.sem, top2.at(p))
                mk = both[:].rearrange("p (b s) e -> p s b e", s=SUB)
                pe.matmul(pos_ps[:, 0:BP * E], before[:], mk[:, 0], start=True, stop=False)
                pe.matmul(pos_ps[:, 0:BP * E], before[:], mk[:, 1], start=False, stop=True)
                pe.matmul(pos_ps[:, BP * E:], upto[:], mk[:, 0], start=True, stop=False)
                pe.matmul(pos_ps[:, BP * E:], before[:], mk[:, 1], start=False, stop=True).then_inc(pos_done.sem, 1)

            def slot(k, m, p, f):
                if m:
                    moe(m, k)
                if k == 0 and f:
                    ctx_transpose(f)
                if k == 1 and p:
                    fc(p, 0)
                    fc(p, 1)
                if k == 2 and f:
                    kv(f, 0)
                if k == 3 and f:
                    x_transpose(f)
                    kv(f, 1)
                if k == 5 and f:
                    q(f, 0)
                if k == 6:
                    if f:
                        q(f, 1)
                    if p:
                        x2_transpose(p, 0)
                        x2_transpose(p, 1)
                if k == 7 and f:
                    q_squares(f)
                    k_transpose(f)
                if k == 8:
                    if p:
                        logits(p)
                    if f:
                        scores(f, 0)
                if k == 9 and f:
                    scores(f, 1)
                    scores(f, 2)
                    scores(f, 3)
                if k == 10 and p:
                    logits_transpose(p)
                if k == 13 and f:
                    p_transpose(f, 0)
                    p_transpose(f, 1)
                    p_transpose(f, 2)
                    p_transpose(f, 3)
                if k == 14:
                    if p:
                        positions(p)
                    if f:
                        attend(f, 0, 0, p)
                if k == 15 and f:
                    attend(f, 0, 1, p)
                    attend(f, 1, 0, p)
                    attend(f, 1, 1, p)

            def fill():
                for f, p in ((Pair(0, 0), None), (Pair(0, 1), Pair(0, 0))):
                    for k in range(SLOTS):
                        if k == 2 and p is None:
                            pe.wait_ge(stage_used, 1)
                            pe.wait_ge(setup_v, ZEROS)
                        if k == 5 and p is None:
                            pe.wait_ge(stage_used, 2)
                        if k == 7 and p is None:
                            pe.wait_ge(setup_v, SETUP_V)
                        if k == 0 and p:
                            pe.wait_ge(stage_used, FRONT_WEIGHTS)
                        slot(k, None, p, f)

            def step(m, p, f, ahead):
                for k in range(SLOTS):
                    slot(k, m, p, f)

            pipeline(pe, fill, step)


INPUTS = ["x", "ctx_1024", "g_xattn", "g_ffn", "L0_xattn_Wq", "L0_xattn_Wkv", "L0_xattn_Wfc",
          "L0_xattn_fc_b", "L0_xattn_qn_w", "L0_xattn_kn_w", "L0_ffn_Wr", "L0_ffn_We"]


def kernel(**inputs):
    import numpy as np
    import concourse.bacc as bacc
    from concourse.bass_utils import run_bass_kernel_spmd

    nc = bacc.Bacc("TRN2", target_bir_lowering=False, num_devices=1)
    arrays, args = {}, []
    for name in INPUTS:
        a = np.ascontiguousarray(inputs[name])
        arrays[f"in_{name}"] = a
        args.append(nc.dram_tensor(f"in_{name}", a.shape, mybir.dt.from_np(a.dtype), kind="ExternalInput").ap())
    out = nc.dram_tensor("out", (B, LQ, D), F32, kind="ExternalOutput").ap()
    build(nc, *args, out)
    result = run_bass_kernel_spmd(nc, [arrays], core_ids=[0])
    return result.results[0]["out"]
```
